# Optimizing a Trainium2 kernel written in Bass

```python
import numpy as np
import jax
import jax.numpy as jnp

def _softmax(x, axis=-1):
    return jax.nn.softmax(x, axis=axis)

def _gelu(x):
    return jax.nn.gelu(x, approximate=True)

def _silu(x):
    return jax.nn.silu(x)

def _sigmoid(x):
    return jax.nn.sigmoid(x)

def _layernorm(x, axis=-1, eps=1e-05):
    m = jnp.mean(x, axis=axis, keepdims=True)
    v = jnp.var(x, axis=axis, keepdims=True)
    return (x - m) / jnp.sqrt(v + eps)

def _scatter_add(tgt, idx, src, axis=0):
    return tgt.at[idx].add(src)

def _segment_sum(src, seg, n):
    return jax.ops.segment_sum(src, seg, n)
kernel_name = 'mk_dlrm_tower_d1_rec_r8_b6b7fd'

def setup_inputs(seed: int=0):
    np.random.seed(seed)
    _w = jnp.asarray

    def _rec_inputs():
        import jax
        import jax.numpy as jnp
        _tk = jax.random.key(seed)
        dense_ctx = jax.random.normal(jax.random.fold_in(_tk, 190), (1024, 16), jnp.float32)
        ids = jnp.stack([jax.random.randint(jax.random.fold_in(_tk, 200 + f), (1024,), 0, v, jnp.int32) for f, v in enumerate([1250, 1000, 1250, 12500, 12500, 1250, 12500, 125000, 1000, 12500, 1000, 1000, 12500, 12500, 12500, 1250, 125000, 125000, 12500, 125000, 12500, 1250, 1250, 1250, 1000, 12500, 1250, 12500, 125000, 125000, 125000, 1250])], axis=1)
        tbl_0 = 0.05 * jax.random.normal(jax.random.fold_in(_tk, 500 + 0), (1250, 16), jnp.float32)
        tbl_1 = 0.05 * jax.random.normal(jax.random.fold_in(_tk, 500 + 1), (1000, 16), jnp.float32)
        tbl_2 = 0.05 * jax.random.normal(jax.random.fold_in(_tk, 500 + 2), (1250, 16), jnp.float32)
        tbl_3 = 0.05 * jax.random.normal(jax.random.fold_in(_tk, 500 + 3), (12500, 16), jnp.float32)
        tbl_4 = 0.05 * jax.random.normal(jax.random.fold_in(_tk, 500 + 4), (12500, 16), jnp.float32)
        tbl_5 = 0.05 * jax.random.normal(jax.random.fold_in(_tk, 500 + 5), (1250, 16), jnp.float32)
        tbl_6 = 0.05 * jax.random.normal(jax.random.fold_in(_tk, 500 + 6), (12500, 16), jnp.float32)
        tbl_7 = 0.05 * jax.random.normal(jax.random.fold_in(_tk, 500 + 7), (125000, 16), jnp.float32)
        tbl_8 = 0.05 * jax.random.normal(jax.random.fold_in(_tk, 500 + 8), (1000, 16), jnp.float32)
        tbl_9 = 0.05 * jax.random.normal(jax.random.fold_in(_tk, 500 + 9), (12500, 16), jnp.float32)
        tbl_10 = 0.05 * jax.random.normal(jax.random.fold_in(_tk, 500 + 10), (1000, 16), jnp.float32)
        tbl_11 = 0.05 * jax.random.normal(jax.random.fold_in(_tk, 500 + 11), (1000, 16), jnp.float32)
        tbl_12 = 0.05 * jax.random.normal(jax.random.fold_in(_tk, 500 + 12), (12500, 16), jnp.float32)
        tbl_13 = 0.05 * jax.random.normal(jax.random.fold_in(_tk, 500 + 13), (12500, 16), jnp.float32)
        tbl_14 = 0.05 * jax.random.normal(jax.random.fold_in(_tk, 500 + 14), (12500, 16), jnp.float32)
        tbl_15 = 0.05 * jax.random.normal(jax.random.fold_in(_tk, 500 + 15), (1250, 16), jnp.float32)
        tbl_16 = 0.05 * jax.random.normal(jax.random.fold_in(_tk, 500 + 16), (125000, 16), jnp.float32)
        tbl_17 = 0.05 * jax.random.normal(jax.random.fold_in(_tk, 500 + 17), (125000, 16), jnp.float32)
        tbl_18 = 0.05 * jax.random.normal(jax.random.fold_in(_tk, 500 + 18), (12500, 16), jnp.float32)
        tbl_19 = 0.05 * jax.random.normal(jax.random.fold_in(_tk, 500 + 19), (125000, 16), jnp.float32)
        tbl_20 = 0.05 * jax.random.normal(jax.random.fold_in(_tk, 500 + 20), (12500, 16), jnp.float32)
        tbl_21 = 0.05 * jax.random.normal(jax.random.fold_in(_tk, 500 + 21), (1250, 16), jnp.float32)
        tbl_22 = 0.05 * jax.random.normal(jax.random.fold_in(_tk, 500 + 22), (1250, 16), jnp.float32)
        tbl_23 = 0.05 * jax.random.normal(jax.random.fold_in(_tk, 500 + 23), (1250, 16), jnp.float32)
        tbl_24 = 0.05 * jax.random.normal(jax.random.fold_in(_tk, 500 + 24), (1000, 16), jnp.float32)
        tbl_25 = 0.05 * jax.random.normal(jax.random.fold_in(_tk, 500 + 25), (12500, 16), jnp.float32)
        tbl_26 = 0.05 * jax.random.normal(jax.random.fold_in(_tk, 500 + 26), (1250, 16), jnp.float32)
        tbl_27 = 0.05 * jax.random.normal(jax.random.fold_in(_tk, 500 + 27), (12500, 16), jnp.float32)
        tbl_28 = 0.05 * jax.random.normal(jax.random.fold_in(_tk, 500 + 28), (125000, 16), jnp.float32)
        tbl_29 = 0.05 * jax.random.normal(jax.random.fold_in(_tk, 500 + 29), (125000, 16), jnp.float32)
        tbl_30 = 0.05 * jax.random.normal(jax.random.fold_in(_tk, 500 + 30), (125000, 16), jnp.float32)
        tbl_31 = 0.05 * jax.random.normal(jax.random.fold_in(_tk, 500 + 31), (1250, 16), jnp.float32)
        _rk = jax.random.fold_in(_tk, 7)
        W_top1 = 0.0606339 * jax.random.normal(jax.random.fold_in(_tk, 801), (272, 512), jnp.float32)
        W_top2 = 0.0441942 * jax.random.normal(jax.random.fold_in(_tk, 802), (512, 256), jnp.float32)
        W_top3 = 0.0625 * jax.random.normal(jax.random.fold_in(_tk, 803), (256, 1), jnp.float32)
        b_top1 = jnp.zeros((512,), jnp.float32)
        b_top2 = jnp.zeros((256,), jnp.float32)
        return (dense_ctx, ids, tbl_0, tbl_1, tbl_2, tbl_3, tbl_4, tbl_5, tbl_6, tbl_7, tbl_8, tbl_9, tbl_10, tbl_11, tbl_12, tbl_13, tbl_14, tbl_15, tbl_16, tbl_17, tbl_18, tbl_19, tbl_20, tbl_21, tbl_22, tbl_23, tbl_24, tbl_25, tbl_26, tbl_27, tbl_28, tbl_29, tbl_30, tbl_31, W_top1, b_top1, W_top2, b_top2, W_top3)
    dense_ctx, ids, tbl_0, tbl_1, tbl_2, tbl_3, tbl_4, tbl_5, tbl_6, tbl_7, tbl_8, tbl_9, tbl_10, tbl_11, tbl_12, tbl_13, tbl_14, tbl_15, tbl_16, tbl_17, tbl_18, tbl_19, tbl_20, tbl_21, tbl_22, tbl_23, tbl_24, tbl_25, tbl_26, tbl_27, tbl_28, tbl_29, tbl_30, tbl_31, W_top1, b_top1, W_top2, b_top2, W_top3 = _rec_inputs()

    def _L0_rec_setup():
        import jax, jax.numpy as jnp
        import numpy as np
        NUM_FIELDS = 32
        EMBED_DIM = 16
        BATCH = 512
        CROSS_SIZES = [128, 128, 128]

        def _cin_forward(x, Ws, bs):
            x0 = x
            h = x
            xs = []
            n_layers = len(Ws)
            for i in range(n_layers):
                B, F, E = x0.shape
                G = h.shape[1]
                z = (x0[:, :, None, :] * h[:, None, :, :]).reshape(B, F * G, E)
                y = jax.nn.relu(jnp.einsum('oc,bce->boe', Ws[i], z) + bs[i][None, :, None])
                if i != n_layers - 1:
                    half = y.shape[1] // 2
                    x_keep, h = (y[:, :half, :], y[:, half:, :])
                else:
                    x_keep, h = (y, y)
                xs.append(x_keep)
            return jnp.sum(jnp.concatenate(xs, axis=1), axis=2)
        key = jax.random.key(seed)
        ks = jax.random.split(key, 8)
        x = jax.random.normal(ks[0], (BATCH, NUM_FIELDS, EMBED_DIM), dtype=jnp.float32)
        prev = NUM_FIELDS
        inp = {'x': x}
        for i, cs in enumerate(CROSS_SIZES):
            in_ch = NUM_FIELDS * prev
            scale = 1.0 / np.sqrt(in_ch)
            inp[f'W{i}'] = jax.random.uniform(ks[1 + 2 * i], (cs, in_ch), dtype=jnp.float32, minval=-scale, maxval=scale)
            inp[f'b{i}'] = jax.random.uniform(ks[2 + 2 * i], (cs,), dtype=jnp.float32, minval=-scale, maxval=scale)
            prev = cs // 2
        return inp
    _L0_rec_all = _L0_rec_setup()
    _L0_rec_in = {k: v for k, v in _L0_rec_all.items() if k in ('W0', 'b0', 'W1', 'b1', 'W2', 'b2')}
    del _L0_rec_all
    return {'dense_ctx': dense_ctx, 'ids': ids, 'tbl_0': tbl_0, 'tbl_1': tbl_1, 'tbl_2': tbl_2, 'tbl_3': tbl_3, 'tbl_4': tbl_4, 'tbl_5': tbl_5, 'tbl_6': tbl_6, 'tbl_7': tbl_7, 'tbl_8': tbl_8, 'tbl_9': tbl_9, 'tbl_10': tbl_10, 'tbl_11': tbl_11, 'tbl_12': tbl_12, 'tbl_13': tbl_13, 'tbl_14': tbl_14, 'tbl_15': tbl_15, 'tbl_16': tbl_16, 'tbl_17': tbl_17, 'tbl_18': tbl_18, 'tbl_19': tbl_19, 'tbl_20': tbl_20, 'tbl_21': tbl_21, 'tbl_22': tbl_22, 'tbl_23': tbl_23, 'tbl_24': tbl_24, 'tbl_25': tbl_25, 'tbl_26': tbl_26, 'tbl_27': tbl_27, 'tbl_28': tbl_28, 'tbl_29': tbl_29, 'tbl_30': tbl_30, 'tbl_31': tbl_31, 'W_top1': W_top1, 'b_top1': b_top1, 'W_top2': W_top2, 'b_top2': b_top2, 'W_top3': W_top3, 'L0_rec_W0': _L0_rec_in['W0'], 'L0_rec_b0': _L0_rec_in['b0'], 'L0_rec_W1': _L0_rec_in['W1'], 'L0_rec_b1': _L0_rec_in['b1'], 'L0_rec_W2': _L0_rec_in['W2'], 'L0_rec_b2': _L0_rec_in['b2']}

def reference(dense_ctx, ids, tbl_0, tbl_1, tbl_2, tbl_3, tbl_4, tbl_5, tbl_6, tbl_7, tbl_8, tbl_9, tbl_10, tbl_11, tbl_12, tbl_13, tbl_14, tbl_15, tbl_16, tbl_17, tbl_18, tbl_19, tbl_20, tbl_21, tbl_22, tbl_23, tbl_24, tbl_25, tbl_26, tbl_27, tbl_28, tbl_29, tbl_30, tbl_31, W_top1, b_top1, W_top2, b_top2, W_top3, L0_rec_W0, L0_rec_b0, L0_rec_W1, L0_rec_b1, L0_rec_W2, L0_rec_b2):
    import jax
    import jax.numpy as jnp

    def _L0_rec_ref(x, W0, b0, W1, b1, W2, b2):
        import jax, jax.numpy as jnp
        import numpy as np
        NUM_FIELDS = 32
        EMBED_DIM = 16
        BATCH = 512
        CROSS_SIZES = [128, 128, 128]

        def _cin_forward(x, Ws, bs):
            x0 = x
            h = x
            xs = []
            n_layers = len(Ws)
            for i in range(n_layers):
                B, F, E = x0.shape
                G = h.shape[1]
                z = (x0[:, :, None, :] * h[:, None, :, :]).reshape(B, F * G, E)
                y = jax.nn.relu(jnp.einsum('oc,bce->boe', Ws[i], z) + bs[i][None, :, None])
                if i != n_layers - 1:
                    half = y.shape[1] // 2
                    x_keep, h = (y[:, :half, :], y[:, half:, :])
                else:
                    x_keep, h = (y, y)
                xs.append(x_keep)
            return jnp.sum(jnp.concatenate(xs, axis=1), axis=2)
        return _cin_forward(x, [W0, W1, W2], [b0, b1, b2])
    e = jnp.stack([tbl_0[ids[:, 0]], tbl_1[ids[:, 1]], tbl_2[ids[:, 2]], tbl_3[ids[:, 3]], tbl_4[ids[:, 4]], tbl_5[ids[:, 5]], tbl_6[ids[:, 6]], tbl_7[ids[:, 7]], tbl_8[ids[:, 8]], tbl_9[ids[:, 9]], tbl_10[ids[:, 10]], tbl_11[ids[:, 11]], tbl_12[ids[:, 12]], tbl_13[ids[:, 13]], tbl_14[ids[:, 14]], tbl_15[ids[:, 15]], tbl_16[ids[:, 16]], tbl_17[ids[:, 17]], tbl_18[ids[:, 18]], tbl_19[ids[:, 19]], tbl_20[ids[:, 20]], tbl_21[ids[:, 21]], tbl_22[ids[:, 22]], tbl_23[ids[:, 23]], tbl_24[ids[:, 24]], tbl_25[ids[:, 25]], tbl_26[ids[:, 26]], tbl_27[ids[:, 27]], tbl_28[ids[:, 28]], tbl_29[ids[:, 29]], tbl_30[ids[:, 30]], tbl_31[ids[:, 31]]], axis=1)
    z = _L0_rec_ref(e, L0_rec_W0, L0_rec_b0, L0_rec_W1, L0_rec_b1, L0_rec_W2, L0_rec_b2)
    z = z.reshape(z.shape[0], -1)
    h = jnp.concatenate([z, dense_ctx], axis=1)
    h = jnp.maximum(h @ W_top1 + b_top1, 0.0)
    h = jnp.maximum(h @ W_top2 + b_top2, 0.0)
    y = h @ W_top3
    return y

_drawn_inputs = setup_inputs


def setup_inputs(seed=0):
    import zlib

    import numpy as np

    out = dict(_drawn_inputs(seed))
    spreads = {'b_top1': (0.0, 0.362), 'b_top2': (0.0, 0.4)}
    factors = {'tbl_0': 8.0,
     'tbl_1': 8.0,
     'tbl_2': 8.0,
     'tbl_3': 8.0,
     'tbl_4': 8.0,
     'tbl_5': 8.0,
     'tbl_6': 8.0,
     'tbl_7': 8.0,
     'tbl_8': 8.0,
     'tbl_9': 8.0,
     'tbl_10': 8.0,
     'tbl_11': 8.0,
     'tbl_12': 8.0,
     'tbl_13': 8.0,
     'tbl_14': 8.0,
     'tbl_15': 8.0,
     'tbl_16': 8.0,
     'tbl_17': 8.0,
     'tbl_18': 8.0,
     'tbl_19': 8.0,
     'tbl_20': 8.0,
     'tbl_21': 8.0,
     'tbl_22': 8.0,
     'tbl_23': 8.0,
     'tbl_24': 8.0,
     'tbl_25': 8.0,
     'tbl_26': 8.0,
     'tbl_27': 8.0,
     'tbl_28': 8.0,
     'tbl_29': 8.0,
     'tbl_30': 8.0,
     'tbl_31': 8.0,
     'L0_rec_W0': 8.0,
     'L0_rec_W1': 8.0,
     'L0_rec_W2': 8.0,
     'L0_rec_b0': 5.019,
     'L0_rec_b1': 7.253,
     'L0_rec_b2': 7.407}
    for name, (base, spread) in spreads.items():
        noise = np.random.default_rng([zlib.crc32(name.encode()), seed]).standard_normal(out[name].shape)
        drawn = base * np.exp(spread * noise) if base else spread * noise
        out[name] = jnp.asarray(drawn.astype(out[name].dtype))
    for name, factor in factors.items():
        out[name] = (out[name] * factor).astype(out[name].dtype)
    return out
```

```python
from contextlib import ExitStack

import concourse.bass as bass
from concourse import mybir

F32 = mybir.dt.float32
F32R = mybir.dt.float32r
I32 = mybir.dt.int32
ALU = mybir.AluOpType
ACT = mybir.ActivationFunctionType

FIELDS, EMB, BATCH, P = 32, 16, 1024, 128
HALF = 64
BLOCKS = BATCH // P
CHUNK = 512
CHUNK_E = CHUNK // P
ITERS = BLOCKS * EMB // (2 * CHUNK_E)
PAIRS = FIELDS // 4
DENSE = 16
TOP1, TOP2 = 512, 256

SPLIT_POOL = (0, 3, 5)
SPLIT_DVE = (1, 6)
SPLIT = tuple(sorted(SPLIT_POOL + SPLIT_DVE))
NATIVE = tuple(i for i in range(PAIRS) if i not in SPLIT)
DVE_ORDER = ("z0", "z1", "z2", "z3", "d1", "z4", "z5", "z6", "z7", "d6")
PE_ORDER = ("N2", "H0", "H1", "L0", "L1", "H3", "N4", "H5", "L3", "H6", "N7", "L5", "L6")

Z_RING = 6
S_RING = 4

GROUPS = 4
Z_ITEMS = GROUPS * PAIRS + 2 * 3
PE_ITEMS = GROUPS * len(PE_ORDER) + 2 * 3
HI_ITEMS = GROUPS * len(SPLIT) + 2
LO_DVE_ITEMS = GROUPS * len(SPLIT_DVE) + 2
LO_POOL_ITEMS = GROUPS * len(SPLIT_POOL)
SEL_ITEMS = 6
H_ITEMS = 4
Y_ITEMS = 6
H_AT = {"0B": 0, "1A": 1, "1B": 2, "0A": 3}
Y_AT = {"0B": 0, "1A": 1, "1B": 2, "2A": 3, "2B": 4, "0A": 5}


def nth(it, per_iteration, k):
    return it * per_iteration + per_iteration + k + 1


def z_item(group, i):
    return group * PAIRS + i


def z0_item(chunk, i):
    return GROUPS * PAIRS + 3 * chunk + i


def pe_item(group, name):
    return group * len(PE_ORDER) + PE_ORDER.index(name)


def pe0_item(chunk, i):
    return GROUPS * len(PE_ORDER) + 3 * chunk + i


def hi_item(group, i):
    return group * len(SPLIT) + SPLIT.index(i)


def hi0_item(chunk):
    return GROUPS * len(SPLIT) + chunk


def lo_dve_item(group, i):
    order = [int(x[1:]) for x in DVE_ORDER if x[0] == "d"]
    return group * len(SPLIT_DVE) + order.index(i)


def lo_dve0_item(chunk):
    return GROUPS * len(SPLIT_DVE) + chunk


def lo_pool_item(group, i):
    return group * len(SPLIT_POOL) + SPLIT_POOL.index(i)


def build(nc, dense_t, ids_d, tables, w0_d, w0m_d, w16_d, w16m_d, w_split_d, w_native_d, bias_d,
          top_w1, top_b1, top_w2, top_b2, top_w3, out_d):
    with ExitStack() as ctx:
        def sb(name, shape, dt=F32):
            return ctx.enter_context(nc.sbuf_tensor(name, shape, dt))

        def ps(name, shape):
            return ctx.enter_context(nc.psum_tensor(name, shape, F32))

        def sem(name):
            return ctx.enter_context(nc.semaphore(name))

        NS, NN = len(SPLIT), len(NATIVE)
        ids_all = sb("ids_all", [P, BLOCKS, FIELDS], I32)
        ids_now = sb("ids_now", [P, FIELDS], I32)
        gathered = sb("gathered", [P, FIELDS, EMB])
        g4 = sb("g4", [P, EMB, P])
        ident = sb("ident", [P, P])
        sel_f = sb("sel_f", [HALF, 5 * P])
        sel = sb("sel", [HALF, 5, P], F32R)
        x4 = [sb(f"x4_{h}", [P, 2 * CHUNK]) for h in range(2)]
        xhl = [sb(f"xhl_{h}", [HALF, 2 * CHUNK], F32R) for h in range(2)]
        xrep = [sb(f"xrep_{c}", [P, FIELDS // 2, CHUNK]) for c in "ab"]
        z_ring = sb("z_ring", [P, Z_RING, 2 * CHUNK])
        zhi = sb("zhi", [P, S_RING, 2 * CHUNK], F32R)
        zlo = sb("zlo", [P, S_RING, 2 * CHUNK], F32R)
        z16 = sb("z16", [96, CHUNK])
        z16s = sb("z16s", [96, CHUNK], F32R)
        w0 = sb("w0", [P, 4, P])
        w16 = sb("w16", [96, P])
        w16s = sb("w16s", [96, P], F32R)
        w_nat = sb("w_nat", [P, 2, 2 * NN, P])
        w_hi = sb("w_hi", [P, 2, 2 * NS, P], F32R)
        w_lo = sb("w_lo", [P, 2, 2 * NS, P], F32R)
        bias = sb("bias", [P, 3])
        kept = [sb(f"kept_{c}", [P, 2, CHUNK]) for c in "ab"]
        esum = sb("esum", [P, 4, 2, P])
        zsum = sb("zsum", [P, 2, BATCH])
        top_a = xrep[0][:, :, :].rearrange("p t n -> p (t n)")
        t1 = top_a[:, 0:3 * TOP1].rearrange("p (k n) -> p k n", k=3)
        t2 = top_a[:, 3 * TOP1:3 * TOP1 + 4 * TOP2].rearrange("p (k n) -> p k n", k=4)
        base = 3 * TOP1 + 4 * TOP2
        t3 = top_a[:, base:base + 2]
        tb1 = top_a[:, base + 2:base + 6]
        tb2 = top_a[:, base + 6:base + 8]
        dense = top_a[0:DENSE, base + 8:base + 8 + BATCH]
        top_b = xrep[1][:, :, :].rearrange("p t n -> p (t n)")
        a1 = top_b[:, 0:4 * BATCH].rearrange("p (k n) -> p k n", k=4)
        a2 = top_b[:, 4 * BATCH:6 * BATCH].rearrange("p (k n) -> p k n", k=2)
        y_out = top_b[0:1, 6 * BATCH:7 * BATCH]
        w_stage = top_b[:, 0:4 * NS * P].rearrange("p (l t o) -> p l t o", l=2, t=2 * NS)
        stage = 4 * NS * P
        w0m = top_b[:, stage:stage + 4 * P].rearrange("p (j o) -> p j o", j=4)
        w16m = top_b[0:96, stage + 4 * P:stage + 5 * P]
        x_dram = [nc.dram_tensor(f"x_dram_{h}", [FIELDS, 2 * CHUNK], F32, kind="Internal").ap()
                  for h in range(2)]

        y = [ps(f"y_{c}", [P, CHUNK]) for c in "ab"]
        h = [ps(f"h_{c}", [P, CHUNK]) for c in "ab"]
        rot = [ps(f"rot_{r}", [P, 2 * CHUNK]) for r in range(2)]

        ids_in = sem("ids_in")
        weights_in = sem("weights_in")
        native_in = sem("native_in")
        memset_done = sem("memset_done")
        consts_ready = sem("consts_ready")
        sel_cast = sem("sel_cast")
        whi_ready = sem("whi_ready")
        wlo_ready = sem("wlo_ready")
        w0_ready = sem("w0_ready")
        ids_copied = sem("ids_copied")
        rows_gathered = sem("rows_gathered")
        g4_ready = sem("g4_ready")
        xt_ready = sem("xt_ready")
        x4_ready = sem("x4_ready")
        xhi_ready = sem("xhi_ready")
        xlo_ready = sem("xlo_ready")
        x_stored = sem("x_stored")
        xrep_in = [[sem(f"xrep_in_{c}{q}") for q in range(4)] for c in "ab"]
        sel_ready = sem("sel_ready")
        z_ready = sem("z_ready")
        hi_ready = sem("hi_ready")
        lo_dve_ready = sem("lo_dve_ready")
        lo_pool_ready = sem("lo_pool_ready")
        pe_done = sem("pe_done")
        h_ready = sem("h_ready")
        y_read = sem("y_read")
        esum_ready = sem("esum_ready")
        zsum_ready = sem("zsum_ready")
        top_in = sem("top_in")
        top_mm = sem("top_mm")
        top_act = sem("top_act")
        out_stored = sem("out_stored")

        def top_bank(n):
            banks = [rot[0][:, 0:CHUNK], rot[0][:, CHUNK:], rot[1][:, 0:CHUNK], rot[1][:, CHUNK:],
                     h[0][:, :], h[1][:, :], y[0][:, :], y[1][:, :]]
            return banks[n]

        block = ctx.enter_context(nc.Block())

        def whole(eng, body):
            with eng.Fori(0, BLOCKS - 1) as m:
                body(2 * m, 0, False)
                body(2 * m + 1, 1, False)
            body(ITERS - 2, 0, False)
            body(ITERS - 1, 1, True)

        @block.sync
        def _(sp):
            sp.dma_start(ids_all[:, :, :], ids_d).then_inc(ids_in, 16)
            sp.dma_start(w_stage, w_split_d).then_inc(weights_in, 16)
            sp.dma_start(w0[:, :, :], w0_d).then_inc(weights_in, 16)
            sp.dma_start(w0m, w0m_d).then_inc(weights_in, 16)
            sp.dma_start(w16[:, :], w16_d).then_inc(weights_in, 16)
            sp.dma_start(w16m, w16m_d).then_inc(weights_in, 16)
            sp.dma_start(w_nat[:, :, :, :], w_native_d).then_inc(native_in, 16)
            sp.dma_start(bias[:, :], bias_d).then_inc(native_in, 16)

            def fetch_x(it, half, first=False):
                sp.wait_ge(x4_ready, it + 1)
                sp.dma_start(x_dram[half], x4[half][0:FIELDS, :]).then_inc(x_stored, 16)
                sp.wait_ge(x_stored, 16 * (it + 1))
                for c in range(2):
                    for q in range(4):
                        if first and c == 1 and q == 0:
                            sp.wait_ge(wlo_ready, 1)
                            sp.wait_ge(whi_ready, 1)
                            sp.wait_ge(w0_ready, 2)
                        if not first:
                            sp.wait_ge(z_ready, nth(it - 1, Z_ITEMS, z_item(2 + c, 2 * q + 1)))
                        for j in range(2):
                            src = bass.AP(tensor=x_dram[half].tensor,
                                          offset=(8 * q + j) * 2 * CHUNK + c * CHUNK,
                                          ap=[[0, HALF], [4 * CHUNK, 4], [1, CHUNK]])
                            sp.dma_start(xrep[c][HALF * j:HALF * (j + 1), 4 * q:4 * q + 4, :],
                                         src).then_inc(xrep_in[c][q], 16)

            fetch_x(0, 0, first=True)

            def body(it, par, last):
                if not last:
                    fetch_x(it + 1, 1 - par)

            whole(sp, body)
            sp.wait_ge(z_ready, nth(ITERS - 1, Z_ITEMS, z_item(2, PAIRS - 1)))
            for k in range(2):
                sp.dma_start(t1[:, k, :], top_w1[k * P:(k + 1) * P, :]).then_inc(top_in, 16)
            sp.dma_start(t1[0:DENSE, 2, :], top_w1[2 * P:2 * P + DENSE, :]).then_inc(top_in, 16)
            sp.dma_start(t2, top_w2.rearrange("(k p) n -> p k n", p=P)).then_inc(top_in, 16)
            sp.dma_start(t3, top_w3).then_inc(top_in, 16)
            sp.dma_start(tb1, top_b1).then_inc(top_in, 16)
            sp.dma_start(tb2, top_b2).then_inc(top_in, 16)
            sp.dma_start(dense, dense_t).then_inc(top_in, 16)
            sp.wait_ge(top_act, 8 + 4 + 2)
            sp.dma_start(out_d.rearrange("n a -> a n"), y_out).then_inc(out_stored, 16)
            sp.wait_ge(out_stored, 16)

        @block.gpsimd
        def _(pool):
            def gather(f0, f1):
                for f in range(f0, f1):
                    nc.gpsimd.indirect_dma_start(
                        out=gathered[:, f, :], out_offset=None, in_=tables[f],
                        in_offset=bass.IndirectOffsetOnAxis(ap=ids_now[:, f:f + 1], axis=0),
                    ).then_inc(rows_gathered, 16)

            def next_ids(blk):
                pool.wait_ge(g4_ready, blk)
                nc.gpsimd.tensor_copy(ids_now[:, :], ids_all[:, blk, :]).then_inc(ids_copied, 1)
                pool.wait_ge(ids_copied, blk + 1)

            pool.sem_inc(lo_pool_ready, LO_POOL_ITEMS)
            pool.wait_ge(ids_in, 16)
            nc.gpsimd.tensor_copy(ids_now[:, :], ids_all[:, 0, :]).then_inc(ids_copied, 1)
            pool.wait_ge(ids_copied, 1)
            gather(0, 8)
            nc.gpsimd.memset(ident[:, :], 0.0).then_inc(memset_done, 1)
            nc.gpsimd.memset(sel_f[:, :], 0.0).then_inc(memset_done, 1)
            pool.wait_ge(memset_done, 2)
            nc.gpsimd.affine_select(out=ident[:, :], in_=ident[:, :], compare_op=ALU.not_equal,
                                    fill=1.0, base=0, pattern=[[-1, P]],
                                    channel_multiplier=1).then_inc(consts_ready, 1)
            main = sel_f[:, 0:4 * P].rearrange("k (j d g) -> k j d g", j=4, d=4)
            rest = sel_f[:, 4 * P:4 * P + 96].rearrange("k (r g) -> k r g", r=3)[:, :, 0:16]
            n = 1
            for wrap in (-FIELDS, 0, FIELDS):
                nc.gpsimd.affine_select(out=main, in_=main, compare_op=ALU.not_equal, fill=1.0,
                                        base=-wrap, pattern=[[-4, 4], [-1, 4], [-1, FIELDS]],
                                        channel_multiplier=1).then_inc(consts_ready, 1)
                n += 1
                pool.wait_ge(consts_ready, n)
            for wrap in (0, FIELDS):
                nc.gpsimd.affine_select(out=rest, in_=rest, compare_op=ALU.not_equal, fill=1.0,
                                        base=-16 - wrap, pattern=[[0, 3], [-1, 16]],
                                        channel_multiplier=1).then_inc(consts_ready, 1)
                n += 1
                pool.wait_ge(consts_ready, n)
            gather(8, FIELDS)
            next_ids(1)
            gather(0, 8)

            def low(it, g, i):
                s = g * NS + SPLIT.index(i)
                pool.wait_ge(hi_ready, nth(it, HI_ITEMS, hi_item(g, i)))
                if s >= S_RING:
                    pg, pi = divmod(s - S_RING, NS)
                    pool.wait_ge(pe_done, nth(it, PE_ITEMS, pe_item(pg, f"L{SPLIT[pi]}")))
                else:
                    pg, pi = divmod(s - S_RING + GROUPS * NS, NS)
                    pool.wait_ge(pe_done, nth(it - 1, PE_ITEMS, pe_item(pg, f"L{SPLIT[pi]}")))
                nc.gpsimd.tensor_tensor(
                    zlo[:, s % S_RING, :], z_ring[:, z_item(g, i) % Z_RING, :],
                    zhi[:, s % S_RING, :].bitcast(F32), ALU.subtract).then_inc(lo_pool_ready, 1)

            def body(it, par, blk, starts=True):
                for g in range(GROUPS):
                    for k, i in enumerate(SPLIT_POOL):
                        low(it, g, i)
                        if par == 1 and g == 2 and k == 0 and starts:
                            next_ids(blk + 2)
                    if par == 0:
                        if blk is not None:
                            gather(8 + 5 * g, 13 + 5 * g)
                    elif g == 0:
                        if blk is not None:
                            gather(28, FIELDS)
                    elif g > 1 and starts:
                        gather(4 * (g - 2), 4 * (g - 1))

            with pool.Fori(0, BLOCKS - 2) as m:
                body(2 * m, 0, m)
                body(2 * m + 1, 1, m)
            body(ITERS - 4, 0, BLOCKS - 2)
            body(ITERS - 3, 1, BLOCKS - 2, starts=False)
            body(ITERS - 2, 0, None)
            body(ITERS - 1, 1, None, starts=False)

        @block.scalar
        def _(act):
            act.sem_inc(hi_ready, HI_ITEMS - 2)
            act.sem_inc(h_ready, H_ITEMS - 1)
            act.sem_inc(y_read, Y_ITEMS - 1)

            def high(it, g, i):
                s = g * NS + SPLIT.index(i)
                act.wait_ge(z_ready, nth(it, Z_ITEMS, z_item(g, i)))
                prev, (pg, pi) = (0, divmod(s - S_RING, NS)) if s >= S_RING else \
                                 (1, divmod(s - S_RING + GROUPS * NS, NS))
                pi = SPLIT[pi]
                act.wait_ge(pe_done, nth(it - prev, PE_ITEMS, pe_item(pg, f"H{pi}")))
                if pi in SPLIT_POOL:
                    act.wait_ge(lo_pool_ready, nth(it - prev, LO_POOL_ITEMS, lo_pool_item(pg, pi)))
                else:
                    act.wait_ge(lo_dve_ready, nth(it - prev, LO_DVE_ITEMS, lo_dve_item(pg, pi)))
                nc.scalar.activation(zhi[:, s % S_RING, :], z_ring[:, z_item(g, i) % Z_RING, :],
                                     ACT.Copy).then_inc(hi_ready, 1)

            def high16(it, c):
                act.wait_ge(z_ready, nth(it, Z_ITEMS, z0_item(c, 2)))
                if c == 0:
                    act.wait_ge(pe_done, nth(it - 1, PE_ITEMS, pe0_item(1, 2)))
                else:
                    act.wait_ge(pe_done, nth(it, PE_ITEMS, pe0_item(0, 2)))
                nc.scalar.activation(z16s[:, :], z16[:, :], ACT.Copy).then_inc(hi_ready, 1)

            def relu0(it, c):
                act.wait_ge(pe_done, nth(it, PE_ITEMS, pe0_item(c, 2)))
                up = slice(HALF, P)
                nc.scalar.activation(h[c][up, :], y[c][up, :], ACT.Relu, bias=bias[up, 0:1])
                nc.scalar.activation(h[c][0:HALF, :], y[c][up, :], ACT.Relu,
                                     bias=bias[up, 0:1]).then_inc(h_ready, 1)
                act.wait_ge(esum_ready, nth(it, 2, c))
                nc.scalar.activation(kept[c][0:HALF, 0, :], y[c][0:HALF, :], ACT.Relu,
                                     bias=bias[0:HALF, 0:1]).then_inc(y_read, 1)

            def relu1(it, c):
                act.wait_ge(pe_done, nth(it, PE_ITEMS, pe_item(c, PE_ORDER[-1])))
                up = slice(HALF, P)
                nc.scalar.activation(h[c][0:HALF, :], y[c][0:HALF, :], ACT.Relu,
                                     bias=bias[0:HALF, 1:2])
                nc.scalar.activation(h[c][up, :], y[c][0:HALF, :], ACT.Relu,
                                     bias=bias[0:HALF, 1:2]).then_inc(h_ready, 1)
                nc.scalar.activation(kept[c][up, 0, :], y[c][up, :], ACT.Relu,
                                     bias=bias[up, 1:2]).then_inc(y_read, 1)

            def relu2(it, c):
                act.wait_ge(pe_done, nth(it, PE_ITEMS, pe_item(2 + c, PE_ORDER[-1])))
                nc.scalar.activation(kept[c][:, 1, :], y[c][:, :], ACT.Relu,
                                     bias=bias[:, 2:3]).then_inc(y_read, 1)

            def spread(blk):
                act.wait_ge(rows_gathered, 16 * FIELDS * (blk + 1))
                for e0 in range(0, EMB, 8):
                    op = nc.scalar.activation(
                        g4[:, e0:e0 + 8, :].rearrange("p e (r f) -> p e r f", r=4),
                        gathered[:, :, e0:e0 + 8].rearrange("p f e -> p e f")[:, :, None, :]
                        .to_broadcast([P, 8, 4, FIELDS]), ACT.Copy)
                op.then_inc(g4_ready, 1)

            def evacuate(it, half):
                act.wait_ge(xt_ready, it + 1)
                nc.scalar.activation(x4[half][:, :], rot[1][:, :], ACT.Copy).then_inc(x4_ready, 1)
                nc.scalar.activation(xhl[half][:, :], rot[1][0:HALF, :],
                                     ACT.Copy).then_inc(xhi_ready, 1)

            act.wait_ge(weights_in, 5 * 16)
            nc.scalar.activation(w_hi[:, :, :, :], w_stage, ACT.Copy).then_inc(whi_ready, 1)
            act.wait_ge(w0_ready, 2)
            nc.scalar.activation(w16s[:, :], w16[:, :], ACT.Copy).then_inc(whi_ready, 1)
            act.wait_ge(consts_ready, 6)
            nc.scalar.activation(sel[:, :, :].rearrange("k j m -> k (j m)"), sel_f[:, :],
                                 ACT.Copy).then_inc(sel_cast, 1)
            act.wait_ge(native_in, 32)
            spread(0)
            evacuate(0, 0)
            high16(-1, 0)
            relu0(-1, 0)
            high16(-1, 1)

            def body(it, par, last):
                for g in range(GROUPS):
                    for k, i in enumerate(SPLIT):
                        if k == 2:
                            if g == 0:
                                relu0(it - 1, 1)
                            elif g < 3:
                                relu1(it, g - 1)
                            else:
                                relu2(it, 0)
                            if g == 2 and not last:
                                evacuate(it + 1, 1 - par)
                        high(it, g, i)
                    if g == 1 and par == 1 and not last:
                        spread_block(it)
                if last:
                    relu2(it, 1)
                else:
                    high16(it, 0)
                    relu2(it, 1)
                    relu0(it, 0)
                    high16(it, 1)

            with act.Fori(0, BLOCKS - 1) as m:
                def spread_block(_, m=m):
                    act.wait_ge(xt_ready, 2 * m + 2)
                    spread(m + 1)
                body(2 * m, 0, False)
                body(2 * m + 1, 1, False)
            body(ITERS - 2, 0, False)
            body(ITERS - 1, 1, True)
            for n in range(2):
                for m in range(4):
                    act.wait_ge(top_mm, 4 * n + m + 1)
                    nc.scalar.activation(a1[:, m, n * CHUNK:(n + 1) * CHUNK], top_bank(4 * n + m),
                                         ACT.Relu, bias=tb1[:, m:m + 1]).then_inc(top_act, 1)
            for n in range(2):
                for m in range(2):
                    act.wait_ge(top_mm, 8 + 2 * n + m + 1)
                    nc.scalar.activation(a2[:, m, n * CHUNK:(n + 1) * CHUNK],
                                         top_bank(2 * n + m), ACT.Relu,
                                         bias=tb2[:, m:m + 1]).then_inc(top_act, 1)
            for n in range(2):
                act.wait_ge(top_mm, 12 + n + 1)
                nc.scalar.activation(y_out[:, n * CHUNK:(n + 1) * CHUNK],
                                     top_bank(4 + n)[0:1, :], ACT.Copy).then_inc(top_act, 1)

        @block.vector
        def _(dve):
            dve.sem_inc(z_ready, Z_ITEMS - 6)
            dve.sem_inc(lo_dve_ready, LO_DVE_ITEMS - 2)
            dve.sem_inc(esum_ready, 2)
            dve.sem_inc(zsum_ready, 1)
            dve.wait_ge(weights_in, 5 * 16)
            nc.vector.tensor_tensor(w0[:, :, :], w0[:, :, :], w0m,
                                    ALU.add).then_inc(w0_ready, 1)
            nc.vector.tensor_tensor(w16[:, :], w16[:, :], w16m,
                                    ALU.add).then_inc(w0_ready, 1)
            dve.wait_ge(whi_ready, 1)
            nc.vector.tensor_tensor(w_lo[:, :, :, :], w_stage, w_hi[:, :, :, :].bitcast(F32),
                                    ALU.subtract).then_inc(wlo_ready, 1)
            dve.wait_ge(whi_ready, 2)
            nc.vector.tensor_tensor(w16s[HALF:96, :], w16[HALF:96, :],
                                    w16s[HALF:96, :].bitcast(F32),
                                    ALU.subtract).then_inc(wlo_ready, 1)

            def slot_free(it, n):
                prev = n < Z_RING
                at = it - 1 if prev else it
                q = n - Z_RING + (Z_ITEMS - 2 if prev else 0)
                if q >= GROUPS * PAIRS:
                    c, i = divmod(q - GROUPS * PAIRS, 2)
                    dve.wait_ge(pe_done, nth(at, PE_ITEMS, pe0_item(c, i)))
                    return
                g, i = divmod(q, PAIRS)
                if i in NATIVE:
                    dve.wait_ge(pe_done, nth(at, PE_ITEMS, pe_item(g, f"N{i}")))
                elif i in SPLIT_POOL:
                    dve.wait_ge(lo_pool_ready, nth(at, LO_POOL_ITEMS, lo_pool_item(g, i)))
                else:
                    dve.wait_ge(lo_dve_ready, nth(at, LO_DVE_ITEMS, lo_dve_item(g, i)))

            def z_pair(it, g, i):
                c = g % 2
                if i == 0:
                    if g < 2:
                        dve.wait_ge(h_ready, nth(it - 1, H_ITEMS, H_AT["0A"]) if g == 0 else
                                    nth(it, H_ITEMS, H_AT["0B"]))
                    else:
                        dve.wait_ge(h_ready, nth(it, H_ITEMS, H_AT["1A" if g == 2 else "1B"]))
                if g < 2 and i % 2 == 0:
                    dve.wait_ge(xrep_in[c][i // 2], 32 * (it + 1))
                slot_free(it, z_item(g, i))
                nc.vector.tensor_tensor(
                    z_ring[:, z_item(g, i) % Z_RING, :].rearrange("p (t n) -> p t n", t=2),
                    xrep[c][:, 2 * i:2 * i + 2, :],
                    h[c][:, None, :].to_broadcast([P, 2, CHUNK]), ALU.mult).then_inc(z_ready, 1)

            def low(it, g, i):
                s = g * NS + SPLIT.index(i)
                dve.wait_ge(hi_ready, nth(it, HI_ITEMS, hi_item(g, i)))
                prev, (pg, pi) = (0, divmod(s - S_RING, NS)) if s >= S_RING else \
                                 (1, divmod(s - S_RING + GROUPS * NS, NS))
                dve.wait_ge(pe_done, nth(it - prev, PE_ITEMS, pe_item(pg, f"L{SPLIT[pi]}")))
                nc.vector.tensor_tensor(
                    zlo[:, s % S_RING, :], z_ring[:, z_item(g, i) % Z_RING, :],
                    zhi[:, s % S_RING, :].bitcast(F32), ALU.subtract).then_inc(lo_dve_ready, 1)

            def z0_pair(it, half, c, i):
                n = GROUPS * PAIRS + 2 * c + i
                dve.wait_ge(sel_ready, nth(it, SEL_ITEMS, 3 * c + i))
                slot_free(it, n)
                nc.vector.tensor_tensor(
                    z_ring[:, n % Z_RING, :].rearrange("p (t n) -> p t n", t=2),
                    rot[i][:, :].rearrange("p (t n) -> p t n", t=2),
                    x4[half][:, None, c * CHUNK:(c + 1) * CHUNK].to_broadcast([P, 2, CHUNK]),
                    ALU.mult).then_inc(z_ready, 1)

            def z0_rest(it, half, c):
                dve.wait_ge(sel_ready, nth(it, SEL_ITEMS, 3 * c + 2))
                if c == 0:
                    dve.wait_ge(lo_dve_ready, nth(it - 1, LO_DVE_ITEMS, lo_dve0_item(1)))
                else:
                    dve.wait_ge(lo_dve_ready, nth(it, LO_DVE_ITEMS, lo_dve0_item(0)))
                nc.vector.tensor_tensor(z16[:, :], rot[0][0:96, 0:CHUNK],
                                        x4[half][0:96, c * CHUNK:(c + 1) * CHUNK],
                                        ALU.mult).then_inc(z_ready, 1)

            def low16(it, c):
                dve.wait_ge(hi_ready, nth(it, HI_ITEMS, hi0_item(c)))
                mid = slice(FIELDS, HALF)
                nc.vector.tensor_tensor(z16s[mid, :], z16[mid, :], z16s[mid, :].bitcast(F32),
                                        ALU.subtract).then_inc(lo_dve_ready, 1)

            def x_low(it, half):
                dve.wait_ge(xhi_ready, it + 1)
                mid = slice(FIELDS, HALF)
                nc.vector.tensor_tensor(xhl[half][mid, :], rot[1][mid, :],
                                        xhl[half][mid, :].bitcast(F32),
                                        ALU.subtract).then_inc(xlo_ready, 1)

            def sum_chunk(it, par, m, c):
                dve.wait_ge(y_read, nth(it, Y_ITEMS, Y_AT["2A" if c == 0 else "2B"]))
                if par == 0 and c == 0:
                    dve.wait_ge(zsum_ready, m + 1)
                nc.vector.tensor_reduce(
                    esum[:, 2 * par + c, :, :],
                    kept[c][:, :, :].rearrange("p k (e b) -> p k b e", b=P),
                    mybir.AxisListType.X, ALU.add).then_inc(esum_ready, 1)

            def sum_block(it, m):
                dve.wait_ge(esum_ready, nth(it, 2, 1))
                nc.vector.tensor_reduce(
                    zsum[:, :, bass.ts(m, P)], esum[:, :, :, :].rearrange("p c k b -> p k b c"),
                    mybir.AxisListType.X, ALU.add).then_inc(zsum_ready, 1)

            def layer0(it, half):
                for c in range(2):
                    z0_pair(it, half, c, 0)
                    z0_pair(it, half, c, 1)
                    z0_rest(it, half, c)
                    low16(it, c)

            x_low(0, 0)
            layer0(-1, 0)

            def body(it, par, m, last):
                for g in range(GROUPS):
                    for item in DVE_ORDER:
                        i = int(item[1:])
                        if item[0] == "z":
                            z_pair(it, g, i)
                        else:
                            low(it, g, i)
                        if g == 2 and i == 3 and not last:
                            x_low(it + 1, 1 - par)
                        if g == 3 and item == "z5":
                            sum_chunk(it, par, m, 0)
                if not last:
                    layer0(it, 1 - par)
                sum_chunk(it, par, m, 1)
                if par == 1:
                    sum_block(it, m)

            with dve.Fori(0, BLOCKS - 1) as m:
                body(2 * m, 0, m, False)
                body(2 * m + 1, 1, m, False)
            body(ITERS - 2, 0, BLOCKS - 1, False)
            body(ITERS - 1, 1, BLOCKS - 1, True)

        @block.tensor
        def _(pe):
            pe.sem_inc(pe_done, PE_ITEMS - 6)

            def transpose_x(it, half):
                for k in range(2 * CHUNK_E):
                    op = nc.tensor.matmul(rot[1][:, k * P:(k + 1) * P],
                                          g4[:, 2 * CHUNK_E * half + k, :], ident[:, :],
                                          start=True, stop=True, is_transpose=True)
                op.then_inc(xt_ready, 1)

            def select(it, half, c, i):
                cols = slice(c * CHUNK, (c + 1) * CHUNK)
                if i < 2:
                    for k in range(2):
                        op = nc.tensor.matmul(rot[i][:, k * CHUNK:(k + 1) * CHUNK],
                                              sel[:, 2 * i + k, :], xhl[half][:, cols],
                                              start=True, stop=True)
                else:
                    op = nc.tensor.matmul(rot[0][:, 0:CHUNK], sel[:, 4, :], xhl[half][:, cols],
                                          start=True, stop=True)
                op.then_inc(sel_ready, 1)

            def layer0_pair(it, c, i):
                n = GROUPS * PAIRS + 2 * c + i
                if i == 0:
                    pe.wait_ge(y_read, nth(it, Y_ITEMS, Y_AT["2A" if c == 0 else "2B"]))
                pe.wait_ge(z_ready, nth(it, Z_ITEMS, z0_item(c, i)))
                for k in range(2):
                    op = nc.tensor.matmul(y[c][:, :], w0[:, 2 * i + k, :],
                                          z_ring[:, n % Z_RING, k * CHUNK:(k + 1) * CHUNK],
                                          start=(i == 0 and k == 0), stop=False)
                op.then_inc(pe_done, 1)

            def layer0_rest(it, c):
                pe.wait_ge(lo_dve_ready, nth(it, LO_DVE_ITEMS, lo_dve0_item(c)))
                nc.tensor.matmul(y[c][:, :], w16s[:, :], z16s[:, :], start=False,
                                 stop=True).then_inc(pe_done, 1)

            def layer0(it, half):
                layer0_pair(it, 0, 0)
                pe.wait_ge(z_ready, nth(it, Z_ITEMS, z0_item(0, 2)))
                select(it, half, 1, 0)
                layer0_pair(it, 0, 1)
                select(it, half, 1, 1)
                layer0_rest(it, 0)
                pe.wait_ge(z_ready, nth(it, Z_ITEMS, z0_item(1, 0)))
                select(it, half, 1, 2)
                layer0_pair(it, 1, 0)
                layer0_pair(it, 1, 1)
                layer0_rest(it, 1)

            def group_item(it, g, item):
                kind, i = item[0], int(item[1:])
                layer, c = divmod(g, 2)
                slot = z_item(g, i) % Z_RING
                first, final = item == PE_ORDER[0], item == PE_ORDER[-1]
                if first:
                    pe.wait_ge(y_read, nth(it - 1, Y_ITEMS, Y_AT["0A"]) if g == 0 else
                               nth(it, Y_ITEMS, Y_AT[("0B", "1A", "1B")[g - 1]]))
                if kind == "N":
                    pe.wait_ge(z_ready, nth(it, Z_ITEMS, z_item(g, i)))
                    n = NATIVE.index(i)
                    terms = [(w_nat[:, layer, 2 * n + k, :], z_ring, slot, k) for k in range(2)]
                else:
                    n = SPLIT.index(i)
                    s = (g * NS + n) % S_RING
                    if kind == "H":
                        pe.wait_ge(hi_ready, nth(it, HI_ITEMS, hi_item(g, i)))
                        terms = [(w[:, layer, 2 * n + k, :], zhi, s, k)
                                 for k in range(2) for w in (w_hi, w_lo)]
                    else:
                        if i in SPLIT_POOL:
                            pe.wait_ge(lo_pool_ready,
                                       nth(it, LO_POOL_ITEMS, lo_pool_item(g, i)))
                        else:
                            pe.wait_ge(lo_dve_ready, nth(it, LO_DVE_ITEMS, lo_dve_item(g, i)))
                        terms = [(w_hi[:, layer, 2 * n + k, :], zlo, s, k) for k in range(2)]
                for t, (w, ring, s, k) in enumerate(terms):
                    op = nc.tensor.matmul(y[c][:, :], w, ring[:, s, k * CHUNK:(k + 1) * CHUNK],
                                          start=(first and t == 0),
                                          stop=(final and t == len(terms) - 1))
                op.then_inc(pe_done, 1)

            pe.wait_ge(consts_ready, 1)
            pe.wait_ge(g4_ready, 1)
            transpose_x(0, 0)
            pe.wait_ge(sel_cast, 1)
            pe.wait_ge(xlo_ready, 1)
            select(-1, 0, 0, 0)
            pe.wait_ge(x4_ready, 1)
            select(-1, 0, 0, 1)
            pe.wait_ge(z_ready, nth(-1, Z_ITEMS, z0_item(0, 0)))
            select(-1, 0, 0, 2)
            pe.wait_ge(w0_ready, 2)
            pe.wait_ge(wlo_ready, 2)
            layer0(-1, 0)
            pe.wait_ge(native_in, 32)

            def body(it, par, m, last):
                nxt = 1 - par
                for g in range(GROUPS):
                    for k, item in enumerate(PE_ORDER):
                        group_item(it, g, item)
                        if g == 3 and k == 5 and not last:
                            pe.wait_ge(xlo_ready, it + 2)
                            select(it, nxt, 0, 0)
                            select(it, nxt, 0, 1)
                        if g == 3 and k == 11 and not last:
                            pe.wait_ge(z_ready, nth(it, Z_ITEMS, z0_item(0, 0)))
                            select(it, nxt, 0, 2)
                    if g == 1 and not last:
                        pe.wait_ge(g4_ready, m + 1 + par)
                        transpose_x(it + 1, nxt)
                if not last:
                    layer0(it, nxt)

            with pe.Fori(0, BLOCKS - 1) as m:
                body(2 * m, 0, m, False)
                body(2 * m + 1, 1, m, False)
            body(ITERS - 2, 0, BLOCKS - 1, False)
            body(ITERS - 1, 1, BLOCKS - 1, True)

            pe.wait_ge(top_in, 8 * 16)
            for n in range(2):
                cols = slice(n * CHUNK, (n + 1) * CHUNK)
                pe.wait_ge(zsum_ready, 1 + (n + 1) * BLOCKS // 2)
                for m in range(4):
                    out = slice(m * P, (m + 1) * P)
                    if n == 1 and m == 2:
                        pe.wait_ge(y_read, nth(ITERS - 1, Y_ITEMS, Y_AT["2B"]))
                    bank = top_bank(4 * n + m)
                    nc.tensor.matmul(bank, t1[:, 0, out], zsum[:, 0, cols], start=True, stop=False)
                    nc.tensor.matmul(bank, t1[:, 1, out], zsum[:, 1, cols], start=False, stop=False)
                    nc.tensor.matmul(bank, t1[0:DENSE, 2, out], dense[:, cols], start=False,
                                     stop=True).then_inc(top_mm, 1)
            for n in range(2):
                cols = slice(n * CHUNK, (n + 1) * CHUNK)
                pe.wait_ge(top_act, 4 * n + 4)
                for m in range(2):
                    for k in range(4):
                        op = nc.tensor.matmul(top_bank(2 * n + m), t2[:, k, m * P:(m + 1) * P],
                                              a1[:, k, cols], start=(k == 0), stop=(k == 3))
                    op.then_inc(top_mm, 1)
            for n in range(2):
                cols = slice(n * CHUNK, (n + 1) * CHUNK)
                pe.wait_ge(top_act, 8 + 2 * n + 2)
                for k in range(2):
                    op = nc.tensor.matmul(top_bank(4 + n)[0:1, :], t3[:, k:k + 1], a2[:, k, cols],
                                          start=(k == 0), stop=(k == 1))
                op.then_inc(top_mm, 1)


def kernel(**inputs):
    import numpy as np
    import concourse.bacc as bacc
    from concourse.bass_utils import run_bass_kernel_spmd

    a = {k: np.asarray(v) for k, v in inputs.items()}
    swap = np.r_[HALF:P, 0:HALF]
    g = np.arange(FIELDS)
    d = np.arange(16)
    w0 = a["L0_rec_W0"].reshape(P, FIELDS, FIELDS)
    near = (g[None, :] + d[:, None]) % FIELDS
    rows = np.broadcast_to(g[None, :], near.shape)
    tiles = lambda w: np.ascontiguousarray(
        w.reshape(P, 4, 4, FIELDS).transpose(2, 3, 1, 0).reshape(P, 4, P))
    mirror = w0[:, near, rows].copy()
    mirror[:, 0, :] = 0
    triple = np.zeros((2, 3, FIELDS, P), w0.dtype)
    low = np.arange(16)
    triple[0, :, :16, :] = w0[:, low, low + 16].T
    triple[1, :, :16, :] = w0[:, low + 16, low].T
    w12 = np.stack([a["L0_rec_W1"][swap], a["L0_rec_W2"]])
    w12 = w12.reshape(2, P, FIELDS // 2, P).transpose(3, 0, 2, 1)
    pick = lambda pairs: np.ascontiguousarray(w12[:, :, [2 * i + k for i in pairs for k in (0, 1)]])
    columns = lambda v: np.ascontiguousarray(v.reshape(-1, P).T)
    arrays = {
        "dense_t": np.ascontiguousarray(a["dense_ctx"].T),
        "ids": np.ascontiguousarray(a["ids"].reshape(BLOCKS, P, FIELDS).transpose(1, 0, 2)),
        "w0": tiles(w0[:, rows, near]), "w0m": tiles(mirror),
        "w16": triple[0].reshape(96, P), "w16m": triple[1].reshape(96, P),
        "w_split": pick(SPLIT), "w_native": pick(NATIVE),
        "bias": np.ascontiguousarray(np.stack([a["L0_rec_b0"], a["L0_rec_b1"][swap],
                                               a["L0_rec_b2"]], axis=1)),
        "top_w1": a["W_top1"], "top_b1": columns(a["b_top1"]), "top_w2": a["W_top2"],
        "top_b2": columns(a["b_top2"]), "top_w3": columns(a["W_top3"]),
        **{f"tbl_{f}": a[f"tbl_{f}"] for f in range(FIELDS)},
    }
    nc = bacc.Bacc("TRN2", target_bir_lowering=False, num_devices=1)
    ap = {k: nc.dram_tensor(f"in_{k}", v.shape, mybir.dt.from_np(v.dtype), kind="ExternalInput").ap()
          for k, v in arrays.items()}
    out = nc.dram_tensor("out_y", (BATCH, 1), F32, kind="ExternalOutput").ap()
    build(nc, ap["dense_t"], ap["ids"], [ap[f"tbl_{f}"] for f in range(FIELDS)], ap["w0"],
          ap["w0m"], ap["w16"], ap["w16m"], ap["w_split"], ap["w_native"], ap["bias"],
          ap["top_w1"], ap["top_b1"], ap["top_w2"], ap["top_b2"], ap["top_w3"], out)
    got = run_bass_kernel_spmd(nc, [{f"in_{k}": v for k, v in arrays.items()}], core_ids=[0])
    return got.results[0]["out_y"]
```

```python
from contextlib import ExitStack

import concourse.bass as bass
from concourse import mybir

F32 = mybir.dt.float32
F32R = mybir.dt.float32r
I32 = mybir.dt.int32
ALU = mybir.AluOpType
ACT = mybir.ActivationFunctionType

FIELDS, EMB, BATCH, P = 32, 16, 1024, 128
HALF = 64
BLOCKS = BATCH // P
CHUNK = 512
CHUNK_E = CHUNK // P
ITERS = BLOCKS * EMB // (2 * CHUNK_E)
PAIRS = FIELDS // 4
DENSE = 16
TOP1, TOP2 = 512, 256

SPLIT_POOL = (0, 3, 5)
SPLIT_DVE = (1, 6)
SPLIT = tuple(sorted(SPLIT_POOL + SPLIT_DVE))
NATIVE = tuple(i for i in range(PAIRS) if i not in SPLIT)
DVE_ORDER = ("z0", "z1", "z2", "z3", "d1", "z4", "z5", "z6", "z7", "d6")
PE_ORDER = ("N2", "H0", "H1", "L0", "L1", "H3", "N4", "H5", "L3", "H6", "N7", "L5", "L6")

Z_RING = 6
S_RING = 4
RELU_AFTER = {"1A": 2, "1B": 2, "2A": 2, "2B": 3}

STEPS = ("1A", "1B", "2A", "0A", "2B", "0B")
Z = (PAIRS, 3)
PE = (len(PE_ORDER), 3)
HI = (len(SPLIT), 1)
LO_DVE = (len(SPLIT_DVE), 1)
LO_POOL = (len(SPLIT_POOL), 0)
RING = (PAIRS, 2)
Y = (1, 1)
Z0 = {"rest": 0, 0: 1, 1: 2}
PE0 = {0: 0, 1: 1, "rest": 2}
DVE_LOWS = [int(x[1:]) for x in DVE_ORDER if x[0] == "d"]
H_AT = {"1A": 0, "1B": 1, "0A": 2, "0B": 3}
Y_BANKS = 3


def total(counts):
    return 4 * counts[0] + 2 * counts[1]


def before(step, counts):
    return sum(counts[s[0] == "0"] for s in STEPS[:STEPS.index(step)])


def is_last(it):
    return isinstance(it, int) and it == ITERS - 1


def done(it, counts, step, k=0):
    missing = counts[1] if is_last(it) and step == "2B" else 0
    return (it + 1) * total(counts) + before(step, counts) - missing + k + 1


def h_done(it, step):
    return (it + 1) * 4 + H_AT[step] + 1


def back(it, step, k, counts, n):
    start = before(step, counts) + k - n
    prev = start < 0
    at = start + total(counts) * prev
    for s in STEPS:
        size = counts[s[0] == "0"]
        if at < size:
            if s == "0A" and is_last(it - prev):
                return back(it, step, k - n, counts, n)
            return it - prev, s, at
        at -= size


def build(nc, dense_t, ids_d, tables, w0_d, w0m_d, w16_d, w16m_d, w_split_d, w_native_d, bias_d,
          top_w1, top_b1, top_w2, top_b2, top_w3, out_d):
    with ExitStack() as ctx:
        def sb(name, shape, dt=F32):
            return ctx.enter_context(nc.sbuf_tensor(name, shape, dt))

        def ps(name, shape):
            return ctx.enter_context(nc.psum_tensor(name, shape, F32))

        def sem(name):
            return ctx.enter_context(nc.semaphore(name))

        NS, NN = len(SPLIT), len(NATIVE)
        ids_all = sb("ids_all", [P, BLOCKS, FIELDS], I32)
        ids_now = sb("ids_now", [P, FIELDS], I32)
        gathered = sb("gathered", [P, FIELDS, EMB])
        g4 = sb("g4", [P, EMB, P])
        ident = sb("ident", [P, P])
        x4 = sb("x4", [P, 2 * CHUNK])
        rot = sb("rot", [P, 4, 2 * CHUNK])
        rot16 = sb("rot16", [96, 2 * CHUNK])
        xrep = [sb(f"xrep_{c}", [P, FIELDS // 2, CHUNK]) for c in "ab"]
        z_ring = sb("z_ring", [P, Z_RING, 2 * CHUNK])
        zhi = sb("zhi", [P, S_RING, 2 * CHUNK], F32R)
        zlo = sb("zlo", [P, S_RING, 2 * CHUNK], F32R)
        z16 = sb("z16", [96, CHUNK])
        z16s = sb("z16s", [96, CHUNK], F32R)
        w0 = sb("w0", [P, 4, P])
        w16 = sb("w16", [96, P])
        w16s = sb("w16s", [96, P], F32R)
        w_nat = sb("w_nat", [P, 2, 2 * NN, P])
        w_hi = sb("w_hi", [P, 2, 2 * NS, P], F32R)
        w_lo = sb("w_lo", [P, 2, 2 * NS, P], F32R)
        bias = sb("bias", [P, 3])
        kept = [sb(f"kept_{c}", [P, 2, CHUNK]) for c in "ab"]
        block_sum = sb("block_sum", [P, 2, P])
        zsum = sb("zsum", [P, 2, BATCH])
        top_a = xrep[0][:, :, :].rearrange("p t n -> p (t n)")
        t1 = top_a[:, 0:3 * TOP1].rearrange("p (k n) -> p k n", k=3)
        t2 = top_a[:, 3 * TOP1:3 * TOP1 + 4 * TOP2].rearrange("p (k n) -> p k n", k=4)
        base = 3 * TOP1 + 4 * TOP2
        t3 = top_a[:, base:base + 2]
        tb1 = top_a[:, base + 2:base + 6]
        tb2 = top_a[:, base + 6:base + 8]
        dense = top_a[0:DENSE, base + 8:base + 8 + BATCH]
        top_b = xrep[1][:, :, :].rearrange("p t n -> p (t n)")
        a1 = top_b[:, 0:4 * BATCH].rearrange("p (k n) -> p k n", k=4)
        a2 = top_b[:, 4 * BATCH:6 * BATCH].rearrange("p (k n) -> p k n", k=2)
        y_out = top_b[0:1, 6 * BATCH:7 * BATCH]
        stage = 4 * NS * P
        w_stage = top_b[:, 0:stage].rearrange("p (l t o) -> p l t o", l=2, t=2 * NS)
        w0m = top_b[:, stage:stage + 4 * P].rearrange("p (j o) -> p j o", j=4)
        w16m = top_b[0:96, stage + 4 * P:stage + 5 * P]
        x_dram = [nc.dram_tensor(f"x_dram_{h}", [FIELDS, 2 * CHUNK], F32, kind="Internal").ap()
                  for h in range(2)]

        y = [ps(f"y_{n}", [P, CHUNK]) for n in range(Y_BANKS)]
        h = [ps(f"h_{c}", [P, CHUNK]) for c in "ab"]
        xt = ps("xt", [P, 2 * CHUNK])

        def y_of(step):
            return y[STEPS.index(step) % Y_BANKS]

        def top_bank(n):
            return [xt[:, 0:CHUNK], xt[:, CHUNK:], h[0][:, :], h[1][:, :],
                    y[0][:, :], y[2][:, :], y[1][:, :]][n]

        ids_in = sem("ids_in")
        weights_in = sem("weights_in")
        native_in = sem("native_in")
        memset_done = sem("memset_done")
        ident_ready = sem("ident_ready")
        whi_ready = sem("whi_ready")
        wlo_ready = sem("wlo_ready")
        w0_ready = sem("w0_ready")
        ids_copied = sem("ids_copied")
        rows_gathered = sem("rows_gathered")
        g4_ready = sem("g4_ready")
        xt_ready = sem("xt_ready")
        x4_ready = sem("x4_ready")
        x_stored = sem("x_stored")
        rot_in = sem("rot_in")
        xrep_in = [[sem(f"xrep_in_{c}{q}") for q in range(4)] for c in "ab"]
        z_ready = sem("z_ready")
        hi_ready = sem("hi_ready")
        lo_dve_ready = sem("lo_dve_ready")
        lo_pool_ready = sem("lo_pool_ready")
        pe_done = sem("pe_done")
        h_ready = sem("h_ready")
        y_read = sem("y_read")
        folded = sem("folded")
        sum_ready = sem("sum_ready")
        top_in = sem("top_in")
        top_mm = sem("top_mm")
        top_act = sem("top_act")
        out_stored = sem("out_stored")

        ROTS = 16 + 3
        def slot(step, k):
            return (before(step, (NS, 0)) + k) % S_RING

        def z_pair_of(step, i):
            return z_ring[:, (before(step, RING) + i) % Z_RING, :]

        def low_slot_free(eng, it, step, k):
            at, s, n = back(it, step, k, (NS, 0), S_RING)
            eng.wait_ge(pe_done, done(at, PE, s, PE_ORDER.index(f"L{SPLIT[n]}")))

        def low_made(eng, it, step, i):
            if i in SPLIT_POOL:
                eng.wait_ge(lo_pool_ready, done(it, LO_POOL, step, SPLIT_POOL.index(i)))
            else:
                eng.wait_ge(lo_dve_ready, done(it, LO_DVE, step, DVE_LOWS.index(i)))

        block = ctx.enter_context(nc.Block())

        @block.sync
        def _(sp):
            sp.dma_start(ids_all[:, :, :], ids_d).then_inc(ids_in, 16)
            sp.dma_start(w_stage, w_split_d).then_inc(weights_in, 16)
            sp.dma_start(w0[:, :, :], w0_d).then_inc(weights_in, 16)
            sp.dma_start(w0m, w0m_d).then_inc(weights_in, 16)
            sp.dma_start(w16[:, :], w16_d).then_inc(weights_in, 16)
            sp.dma_start(w16m, w16m_d).then_inc(weights_in, 16)
            sp.dma_start(w_nat[:, :, :, :], w_native_d).then_inc(native_in, 16)
            sp.dma_start(bias[:, :], bias_d).then_inc(native_in, 16)

            def fetch_x(it, half, first=False):
                sp.wait_ge(x4_ready, it + 1)
                sp.dma_start(x_dram[half], x4[0:FIELDS, :]).then_inc(x_stored, 16)
                if not first:
                    sp.wait_ge(z_ready, done(it - 2, Z, "0B", Z0[1]))
                for r in range(3):
                    sp.dma_start(rot16[32 * r:32 * (r + 1), :], x4[16:48, :]).then_inc(rot_in, 16)
                for j in range(4):
                    for d in range(4):
                        sp.dma_start(rot[32 * d:32 * (d + 1), j, :],
                                     x4[4 * j + d:4 * j + d + 32, :]).then_inc(rot_in, 16)
                sp.wait_ge(x_stored, 16 * (it + 1))
                for c in range(2):
                    for q in range(4):
                        if first and c == 1 and q == 0:
                            sp.wait_ge(wlo_ready, 1)
                            sp.wait_ge(whi_ready, 1)
                            sp.wait_ge(w0_ready, 2)
                        if not first:
                            sp.wait_ge(z_ready, done(it - 1, Z, "2" + "AB"[c], 2 * q + 1))
                        for j in range(2):
                            src = bass.AP(tensor=x_dram[half].tensor,
                                          offset=(8 * q + j) * 2 * CHUNK + c * CHUNK,
                                          ap=[[0, HALF], [4 * CHUNK, 4], [1, CHUNK]])
                            sp.dma_start(xrep[c][HALF * j:HALF * (j + 1), 4 * q:4 * q + 4, :],
                                         src).then_inc(xrep_in[c][q], 16)

            fetch_x(0, 0, first=True)
            with sp.Fori(0, BLOCKS - 1) as m:
                fetch_x(2 * m + 1, 1)
                fetch_x(2 * m + 2, 0)
            fetch_x(ITERS - 1, 1)
            sp.wait_ge(z_ready, done(ITERS - 1, Z, "2A", PAIRS - 1))
            for k in range(2):
                sp.dma_start(t1[:, k, :], top_w1[k * P:(k + 1) * P, :]).then_inc(top_in, 16)
            sp.dma_start(t1[0:DENSE, 2, :], top_w1[2 * P:2 * P + DENSE, :]).then_inc(top_in, 16)
            sp.dma_start(t2, top_w2.rearrange("(k p) n -> p k n", p=P)).then_inc(top_in, 16)
            sp.dma_start(t3, top_w3).then_inc(top_in, 16)
            sp.dma_start(tb1, top_b1).then_inc(top_in, 16)
            sp.dma_start(tb2, top_b2).then_inc(top_in, 16)
            sp.dma_start(dense, dense_t).then_inc(top_in, 16)
            sp.wait_ge(top_act, 8 + 4 + 2)
            sp.dma_start(out_d.rearrange("n a -> a n"), y_out).then_inc(out_stored, 16)
            sp.wait_ge(out_stored, 16)

        @block.gpsimd
        def _(pool):
            def gather(f0, f1):
                for f in range(f0, f1):
                    nc.gpsimd.indirect_dma_start(
                        out=gathered[:, f, :], out_offset=None, in_=tables[f],
                        in_offset=bass.IndirectOffsetOnAxis(ap=ids_now[:, f:f + 1], axis=0),
                    ).then_inc(rows_gathered, 16)

            def next_ids(blk):
                pool.wait_ge(g4_ready, 2 * blk)
                nc.gpsimd.tensor_copy(ids_now[:, :], ids_all[:, blk, :]).then_inc(ids_copied, 1)
                pool.wait_ge(ids_copied, blk + 1)

            pool.sem_inc(lo_pool_ready, total(LO_POOL))
            pool.sem_inc(sum_ready, 2)
            pool.wait_ge(ids_in, 16)
            nc.gpsimd.tensor_copy(ids_now[:, :], ids_all[:, 0, :]).then_inc(ids_copied, 1)
            pool.wait_ge(ids_copied, 1)
            gather(0, 8)
            nc.gpsimd.memset(ident[:, :], 0.0).then_inc(memset_done, 1)
            pool.wait_ge(memset_done, 1)
            nc.gpsimd.affine_select(out=ident[:, :], in_=ident[:, :], compare_op=ALU.not_equal,
                                    fill=1.0, base=0, pattern=[[-1, P]],
                                    channel_multiplier=1).then_inc(ident_ready, 1)
            gather(8, FIELDS)
            next_ids(1)
            gather(0, 12)

            def low(it, step, i):
                k = SPLIT.index(i)
                s = slot(step, k)
                pool.wait_ge(hi_ready, done(it, HI, step, k))
                low_slot_free(pool, it, step, k)
                nc.gpsimd.tensor_tensor(zlo[:, s, :], z_pair_of(step, i), zhi[:, s, :].bitcast(F32),
                                        ALU.subtract).then_inc(lo_pool_ready, 1)

            def sum_chunk(it, par, blk, c, folds):
                pool.wait_ge(y_read, done(it, Y, "2" + "AB"[c]))
                v = kept[c]
                nc.gpsimd.tensor_tensor(v[:, :, 0:2 * P], v[:, :, 0:2 * P], v[:, :, 2 * P:4 * P],
                                        ALU.add).then_inc(folded, 1)
                pool.wait_ge(folded, folds + 1)
                if par == 0 and c == 0:
                    pool.wait_ge(sum_ready, 2 * it + 2)
                    nc.gpsimd.tensor_tensor(block_sum[:, :, :], v[:, :, 0:P], v[:, :, P:2 * P],
                                            ALU.add).then_inc(sum_ready, 1)
                    return
                nc.gpsimd.tensor_tensor(v[:, :, 0:P], v[:, :, 0:P], v[:, :, P:2 * P],
                                        ALU.add).then_inc(folded, 1)
                pool.wait_ge(folded, folds + 2)
                pool.wait_ge(sum_ready, 2 * it + 2 + c)
                out = zsum[:, :, bass.ts(blk, P)] if par == 1 and c == 1 else block_sum[:, :, :]
                nc.gpsimd.tensor_tensor(out, block_sum[:, :, :], v[:, :, 0:P],
                                        ALU.add).then_inc(sum_ready, 1)

            ODD = {"1B": (0, 4), "2A": (4, 8), "2B": (8, 12)}
            EVEN = {"1A": (12, 17), "1B": (17, 22), "2A": (22, 27), "2B": (27, FIELDS)}

            def body(it, par, blk, gathers):
                for step in STEPS:
                    if step[0] != "0":
                        for k, i in enumerate(SPLIT_POOL):
                            if k == 2 and step == "1B" and par == 1 and gathers:
                                next_ids(blk + 2)
                            low(it, step, i)
                            if step == "2B" and k == 0:
                                sum_chunk(it, par, blk, 0, 7 * blk + 3 * par)
                    if gathers and step in gathers:
                        gather(*gathers[step])
                sum_chunk(it, par, blk, 1, 7 * blk + 3 * par + 1 + par)

            with pool.Fori(0, BLOCKS - 2) as m:
                body(2 * m, 0, m, EVEN)
                body(2 * m + 1, 1, m, ODD)
            body(ITERS - 4, 0, BLOCKS - 2, EVEN)
            body(ITERS - 3, 1, BLOCKS - 2, None)
            body(ITERS - 2, 0, BLOCKS - 1, None)
            body(ITERS - 1, 1, BLOCKS - 1, None)

        @block.scalar
        def _(act):
            def high(it, step, i):
                k = SPLIT.index(i)
                act.wait_ge(z_ready, done(it, Z, step, i))
                at, s, n = back(it, step, k, (NS, 0), S_RING)
                act.wait_ge(pe_done, done(at, PE, s, PE_ORDER.index(f"H{SPLIT[n]}")))
                low_made(act, at, s, SPLIT[n])
                nc.scalar.activation(zhi[:, slot(step, k), :], z_pair_of(step, i),
                                     ACT.Copy).then_inc(hi_ready, 1)

            def high16(it, step):
                act.wait_ge(z_ready, done(it, Z, step, Z0["rest"]))
                act.wait_ge(pe_done, done(it - (step == "0A"), PE, "0B" if step == "0A" else "0A",
                                          PE0["rest"]))
                nc.scalar.activation(z16s[:, :], z16[:, :], ACT.Copy).then_inc(hi_ready, 1)

            up, down = slice(HALF, P), slice(0, HALF)

            def relu(it, step):
                layer, c = int(step[0]), "AB".index(step[1])
                act.wait_ge(pe_done, done(it, PE, step, PE[layer == 0] - 1))
                yy = y_of(step)
                if layer == 2:
                    nc.scalar.activation(kept[c][:, 1, :], yy[:, :], ACT.Relu,
                                         bias=bias[:, 2:3]).then_inc(y_read, 1)
                    return
                on, off = (up, down) if layer == 0 else (down, up)
                nc.scalar.activation(h[c][on, :], yy[on, :], ACT.Relu, bias=bias[on, layer:layer + 1])
                nc.scalar.activation(h[c][off, :], yy[on, :], ACT.Relu,
                                     bias=bias[on, layer:layer + 1]).then_inc(h_ready, 1)
                if layer == 0:
                    act.wait_ge(sum_ready, 2 * (it + 1) + c + 1)
                nc.scalar.activation(kept[c][off, 0, :], yy[off, :], ACT.Relu,
                                     bias=bias[off, layer:layer + 1]).then_inc(y_read, 1)

            def spread(blk):
                act.wait_ge(rows_gathered, 16 * FIELDS * (blk + 1))
                for e0 in range(0, EMB, 8):
                    nc.scalar.activation(
                        g4[:, e0:e0 + 8, :].rearrange("p e (r f) -> p e r f", r=4),
                        gathered[:, :, e0:e0 + 8].rearrange("p f e -> p e f")[:, :, None, :]
                        .to_broadcast([P, 8, 4, FIELDS]), ACT.Copy).then_inc(g4_ready, 1)

            def evacuate(it):
                act.wait_ge(xt_ready, it + 1)
                nc.scalar.activation(x4[:, :], xt[:, :], ACT.Copy).then_inc(x4_ready, 1)

            act.sem_inc(hi_ready, before("0A", HI))
            act.sem_inc(h_ready, 2)
            act.sem_inc(y_read, 3)
            act.wait_ge(weights_in, 5 * 16)
            nc.scalar.activation(w_hi[:, :, :, :], w_stage, ACT.Copy).then_inc(whi_ready, 1)
            act.wait_ge(w0_ready, 2)
            nc.scalar.activation(w16s[:, :], w16[:, :], ACT.Copy).then_inc(whi_ready, 1)
            act.wait_ge(native_in, 32)
            spread(0)
            evacuate(0)
            high16(-1, "0A")
            act.wait_ge(hi_ready, done(-1, HI, "0A"))
            act.sem_inc(hi_ready, HI[0])
            relu(-1, "0A")
            act.wait_ge(y_read, done(-1, Y, "0A"))
            act.sem_inc(y_read, 1)
            high16(-1, "0B")

            def body(it, par, m, last):
                for step, earlier in zip(STEPS, (None,) + STEPS):
                    if step[0] == "0":
                        if not last:
                            high16(it, step)
                            if step == "0A":
                                relu(it, "2A")
                        elif step == "0A":
                            relu(it, "2A")
                        if step == "0B":
                            relu(it, "2B")
                        continue
                    for k, i in enumerate(SPLIT):
                        if k == RELU_AFTER[step]:
                            if step == "1A":
                                relu(it - 1, "0B")
                            elif step != "2B" or not last:
                                relu(it, earlier)
                            if step == "1B" and not last:
                                evacuate(it + 1)
                        high(it, step, i)
                    if step == "1A" and par == 1 and not last:
                        act.wait_ge(xt_ready, 2 * m + 2)
                        spread(m + 1)

            with act.Fori(0, BLOCKS - 1) as m:
                body(2 * m, 0, m, False)
                body(2 * m + 1, 1, m, False)
            body(ITERS - 2, 0, BLOCKS - 1, False)
            body(ITERS - 1, 1, BLOCKS - 1, True)
            for n in range(2):
                for m in range(4):
                    act.wait_ge(top_mm, 4 * n + m + 1)
                    nc.scalar.activation(a1[:, m, n * CHUNK:(n + 1) * CHUNK],
                                         top_bank((4 * n + m) % 7),
                                         ACT.Relu, bias=tb1[:, m:m + 1]).then_inc(top_act, 1)
            for n in range(2):
                for m in range(2):
                    act.wait_ge(top_mm, 8 + 2 * n + m + 1)
                    nc.scalar.activation(a2[:, m, n * CHUNK:(n + 1) * CHUNK],
                                         top_bank(1 + 2 * n + m), ACT.Relu,
                                         bias=tb2[:, m:m + 1]).then_inc(top_act, 1)
            for n in range(2):
                act.wait_ge(top_mm, 12 + n + 1)
                nc.scalar.activation(y_out[:, n * CHUNK:(n + 1) * CHUNK],
                                     top_bank(5 + n)[0:1, :], ACT.Copy).then_inc(top_act, 1)

        @block.vector
        def _(dve):
            dve.sem_inc(z_ready, before("0A", Z))
            dve.sem_inc(lo_dve_ready, before("0A", LO_DVE))
            dve.wait_ge(weights_in, 5 * 16)
            nc.vector.tensor_tensor(w0[:, :, :], w0[:, :, :], w0m, ALU.add).then_inc(w0_ready, 1)
            nc.vector.tensor_tensor(w16[:, :], w16[:, :], w16m, ALU.add).then_inc(w0_ready, 1)
            dve.wait_ge(whi_ready, 1)
            nc.vector.tensor_tensor(w_lo[:, :, :, :], w_stage, w_hi[:, :, :, :].bitcast(F32),
                                    ALU.subtract).then_inc(wlo_ready, 1)
            dve.wait_ge(whi_ready, 2)
            nc.vector.tensor_tensor(w16s[HALF:96, :], w16[HALF:96, :],
                                    w16s[HALF:96, :].bitcast(F32),
                                    ALU.subtract).then_inc(wlo_ready, 1)

            def slot_free(it, step, i):
                at, s, n = back(it, step, i, RING, Z_RING)
                if s[0] == "0":
                    dve.wait_ge(pe_done, done(at, PE, s, PE0[n]))
                elif n in NATIVE:
                    dve.wait_ge(pe_done, done(at, PE, s, PE_ORDER.index(f"N{n}")))
                else:
                    low_made(dve, at, s, n)

            def z_pair(it, step, i):
                c = "AB".index(step[1])
                if i == 0:
                    dve.wait_ge(h_ready, h_done(it - 1, "0" + step[1]) if step[0] == "1" else
                                h_done(it, "1" + step[1]))
                if step[0] == "1" and i % 2 == 0:
                    dve.wait_ge(xrep_in[c][i // 2], 32 * (it + 1))
                slot_free(it, step, i)
                nc.vector.tensor_tensor(
                    z_pair_of(step, i).rearrange("p (t n) -> p t n", t=2),
                    xrep[c][:, 2 * i:2 * i + 2, :],
                    h[c][:, None, :].to_broadcast([P, 2, CHUNK]), ALU.mult).then_inc(z_ready, 1)

            def low(it, step, i):
                k = SPLIT.index(i)
                s = slot(step, k)
                dve.wait_ge(hi_ready, done(it, HI, step, k))
                low_slot_free(dve, it, step, k)
                nc.vector.tensor_tensor(zlo[:, s, :], z_pair_of(step, i), zhi[:, s, :].bitcast(F32),
                                        ALU.subtract).then_inc(lo_dve_ready, 1)

            def layer0(it, step):
                cols = slice(0, CHUNK) if step == "0A" else slice(CHUNK, 2 * CHUNK)
                if step == "0A":
                    dve.wait_ge(rot_in, 16 * ROTS * (it + 2))
                other = (it - 1, "0B") if step == "0A" else (it, "0A")
                dve.wait_ge(lo_dve_ready, done(other[0], LO_DVE, other[1]))
                nc.vector.tensor_tensor(z16[:, :], rot16[:, cols], x4[0:96, cols],
                                        ALU.mult).then_inc(z_ready, 1)
                for i in range(2):
                    slot_free(it, step, i)
                    nc.vector.tensor_tensor(
                        z_pair_of(step, i).rearrange("p (t n) -> p t n", t=2),
                        rot[:, 2 * i:2 * i + 2, cols],
                        x4[:, None, cols].to_broadcast([P, 2, CHUNK]),
                        ALU.mult).then_inc(z_ready, 1)
                dve.wait_ge(hi_ready, done(it, HI, step))
                mid = slice(FIELDS, HALF)
                nc.vector.tensor_tensor(z16s[mid, :], z16[mid, :], z16s[mid, :].bitcast(F32),
                                        ALU.subtract).then_inc(lo_dve_ready, 1)

            dve.wait_ge(x4_ready, 1)
            layer0(-1, "0A")
            dve.wait_ge(z_ready, done(-1, Z, "0A", 2))
            dve.wait_ge(lo_dve_ready, done(-1, LO_DVE, "0A"))
            dve.sem_inc(z_ready, Z[0])
            dve.sem_inc(lo_dve_ready, LO_DVE[0])
            layer0(-1, "0B")

            def body(it, last):
                for step in STEPS:
                    if step[0] == "0":
                        if not last:
                            layer0(it, step)
                        continue
                    for item in DVE_ORDER:
                        (z_pair if item[0] == "z" else low)(it, step, int(item[1:]))

            with dve.Fori(0, BLOCKS - 1) as m:
                body(2 * m, False)
                body(2 * m + 1, False)
            body(ITERS - 2, False)
            body(ITERS - 1, True)

        @block.tensor
        def _(pe):
            def transpose_x(it, half):
                for k in range(2 * CHUNK_E):
                    op = nc.tensor.matmul(xt[:, k * P:(k + 1) * P],
                                          g4[:, 2 * CHUNK_E * half + k, :], ident[:, :],
                                          start=True, stop=True, is_transpose=True)
                op.then_inc(xt_ready, 1)

            def y_free(it, step):
                at, s, _ = back(it, step, 0, Y, Y_BANKS)
                pe.wait_ge(y_read, done(at, Y, s))

            def layer0(it, step):
                y_free(it, step)
                yy = y_of(step)
                for i in range(2):
                    pe.wait_ge(z_ready, done(it, Z, step, Z0[i]))
                    for k in range(2):
                        op = nc.tensor.matmul(yy[:, :], w0[:, 2 * i + k, :],
                                              z_pair_of(step, i)[:, k * CHUNK:(k + 1) * CHUNK],
                                              start=(i == 0 and k == 0), stop=False)
                    op.then_inc(pe_done, 1)
                pe.wait_ge(lo_dve_ready, done(it, LO_DVE, step))
                nc.tensor.matmul(yy[:, :], w16s[:, :], z16s[:, :], start=False,
                                 stop=True).then_inc(pe_done, 1)

            def item_of(it, step, item):
                kind, i = item[0], int(item[1:])
                layer = int(step[0]) - 1
                first, final = item == PE_ORDER[0], item == PE_ORDER[-1]
                if kind == "N":
                    pe.wait_ge(z_ready, done(it, Z, step, i))
                    n = NATIVE.index(i)
                    terms = [(w_nat[:, layer, 2 * n + k, :], z_pair_of(step, i), k)
                             for k in range(2)]
                else:
                    n = SPLIT.index(i)
                    s = slot(step, n)
                    if kind == "H":
                        pe.wait_ge(hi_ready, done(it, HI, step, n))
                        terms = [(w[:, layer, 2 * n + k, :], zhi[:, s, :], k)
                                 for k in range(2) for w in (w_hi, w_lo)]
                    else:
                        low_made(pe, it, step, i)
                        terms = [(w_hi[:, layer, 2 * n + k, :], zlo[:, s, :], k) for k in range(2)]
                for t, (w, z, k) in enumerate(terms):
                    op = nc.tensor.matmul(y_of(step)[:, :], w, z[:, k * CHUNK:(k + 1) * CHUNK],
                                          start=(first and t == 0),
                                          stop=(final and t == len(terms) - 1))
                op.then_inc(pe_done, 1)

            pe.sem_inc(pe_done, before("0A", PE))
            pe.wait_ge(ident_ready, 1)
            pe.wait_ge(g4_ready, 1)
            transpose_x(0, 0)
            pe.wait_ge(w0_ready, 2)
            pe.wait_ge(wlo_ready, 2)
            layer0(-1, "0A")
            pe.wait_ge(pe_done, done(-1, PE, "0A", 2))
            pe.sem_inc(pe_done, PE[0])
            layer0(-1, "0B")
            pe.wait_ge(native_in, 32)

            def body(it, par, m, last):
                for step in STEPS:
                    if step[0] == "0":
                        if not last:
                            layer0(it, step)
                        continue
                    y_free(it, step)
                    for item in PE_ORDER:
                        item_of(it, step, item)
                    if step == "1A" and not last:
                        pe.wait_ge(g4_ready, 2 * (m + par) + 2 - par)
                        transpose_x(it + 1, 1 - par)

            with pe.Fori(0, BLOCKS - 1) as m:
                body(2 * m, 0, m, False)
                body(2 * m + 1, 1, m, False)
            body(ITERS - 2, 0, BLOCKS - 1, False)
            body(ITERS - 1, 1, BLOCKS - 1, True)

            pe.wait_ge(top_in, 8 * 16)
            for n in range(2):
                cols = slice(n * CHUNK, (n + 1) * CHUNK)
                pe.wait_ge(sum_ready, 2 + (n + 1) * ITERS)
                for m in range(4):
                    out = slice(m * P, (m + 1) * P)
                    if 4 * n + m == 6:
                        pe.wait_ge(y_read, done(ITERS - 1, Y, "2B") - 1)
                    if 4 * n + m == 7:
                        pe.wait_ge(top_act, 1)
                    bank = top_bank((4 * n + m) % 7)
                    nc.tensor.matmul(bank, t1[:, 0, out], zsum[:, 0, cols], start=True, stop=False)
                    nc.tensor.matmul(bank, t1[:, 1, out], zsum[:, 1, cols], start=False, stop=False)
                    nc.tensor.matmul(bank, t1[0:DENSE, 2, out], dense[:, cols], start=False,
                                     stop=True).then_inc(top_mm, 1)
            for n in range(2):
                cols = slice(n * CHUNK, (n + 1) * CHUNK)
                pe.wait_ge(top_act, 4 * n + 4)
                for m in range(2):
                    for k in range(4):
                        op = nc.tensor.matmul(top_bank(1 + 2 * n + m), t2[:, k, m * P:(m + 1) * P],
                                              a1[:, k, cols], start=(k == 0), stop=(k == 3))
                    op.then_inc(top_mm, 1)
            for n in range(2):
                cols = slice(n * CHUNK, (n + 1) * CHUNK)
                pe.wait_ge(top_act, 8 + 2 * n + 2)
                for k in range(2):
                    op = nc.tensor.matmul(top_bank(5 + n)[0:1, :], t3[:, k:k + 1], a2[:, k, cols],
                                          start=(k == 0), stop=(k == 1))
                op.then_inc(top_mm, 1)


def kernel(**inputs):
    import numpy as np
    import concourse.bacc as bacc
    from concourse.bass_utils import run_bass_kernel_spmd

    a = {k: np.asarray(v) for k, v in inputs.items()}
    swap = np.r_[HALF:P, 0:HALF]
    g = np.arange(FIELDS)
    d = np.arange(16)
    w0 = a["L0_rec_W0"].reshape(P, FIELDS, FIELDS)
    near = (g[None, :] + d[:, None]) % FIELDS
    rows = np.broadcast_to(g[None, :], near.shape)
    tiles = lambda w: np.ascontiguousarray(
        w.reshape(P, 4, 4, FIELDS).transpose(2, 3, 1, 0).reshape(P, 4, P))
    mirror = w0[:, near, rows].copy()
    mirror[:, 0, :] = 0
    triple = np.zeros((2, 3, FIELDS, P), w0.dtype)
    low = np.arange(16)
    triple[0, :, :16, :] = w0[:, low, low + 16].T
    triple[1, :, :16, :] = w0[:, low + 16, low].T
    w12 = np.stack([a["L0_rec_W1"][swap], a["L0_rec_W2"]])
    w12 = w12.reshape(2, P, FIELDS // 2, P).transpose(3, 0, 2, 1)
    pick = lambda pairs: np.ascontiguousarray(w12[:, :, [2 * i + k for i in pairs for k in (0, 1)]])
    columns = lambda v: np.ascontiguousarray(v.reshape(-1, P).T)
    arrays = {
        "dense_t": np.ascontiguousarray(a["dense_ctx"].T),
        "ids": np.ascontiguousarray(a["ids"].reshape(BLOCKS, P, FIELDS).transpose(1, 0, 2)),
        "w0": tiles(w0[:, rows, near]), "w0m": tiles(mirror),
        "w16": triple[0].reshape(96, P), "w16m": triple[1].reshape(96, P),
        "w_split": pick(SPLIT), "w_native": pick(NATIVE),
        "bias": np.ascontiguousarray(np.stack([a["L0_rec_b0"], a["L0_rec_b1"][swap],
                                               a["L0_rec_b2"]], axis=1)),
        "top_w1": a["W_top1"], "top_b1": columns(a["b_top1"]), "top_w2": a["W_top2"],
        "top_b2": columns(a["b_top2"]), "top_w3": columns(a["W_top3"]),
        **{f"tbl_{f}": a[f"tbl_{f}"] for f in range(FIELDS)},
    }
    nc = bacc.Bacc("TRN2", target_bir_lowering=False, num_devices=1)
    ap = {k: nc.dram_tensor(f"in_{k}", v.shape, mybir.dt.from_np(v.dtype), kind="ExternalInput").ap()
          for k, v in arrays.items()}
    out = nc.dram_tensor("out_y", (BATCH, 1), F32, kind="ExternalOutput").ap()
    build(nc, ap["dense_t"], ap["ids"], [ap[f"tbl_{f}"] for f in range(FIELDS)], ap["w0"],
          ap["w0m"], ap["w16"], ap["w16m"], ap["w_split"], ap["w_native"], ap["bias"],
          ap["top_w1"], ap["top_b1"], ap["top_w2"], ap["top_b2"], ap["top_w3"], out)
    got = run_bass_kernel_spmd(nc, [{f"in_{k}": v for k, v in arrays.items()}], core_ids=[0])
    return got.results[0]["out_y"]
```

```python
from contextlib import ExitStack

import concourse.bass as bass
from concourse import mybir

F32 = mybir.dt.float32
F32R = mybir.dt.float32r
I32 = mybir.dt.int32
ALU = mybir.AluOpType
ACT = mybir.ActivationFunctionType

FIELDS, EMB, BATCH, P = 32, 16, 1024, 128
HALF = 64
BLOCKS = BATCH // P
CHUNK = 512
CHUNK_E = CHUNK // P
ITERS = BLOCKS * EMB // (2 * CHUNK_E)
PAIRS = FIELDS // 4
DENSE = 16
TOP1, TOP2 = 512, 256

SPLIT_POOL = (0, 3, 5)
SPLIT_DVE = (1, 6)
SPLIT = tuple(sorted(SPLIT_POOL + SPLIT_DVE))
NATIVE = tuple(i for i in range(PAIRS) if i not in SPLIT)
DVE_ORDER = ("z0", "z1", "z2", "z3", "d1", "z4", "z5", "z6", "z7", "d6")
PE_ORDER = ("N2", "H0", "H1", "L1", "L0", "H3", "N4", "H5", "H6", "L3", "N7", "L5", "L6")

Z_RING = 6
S_RING = 4
RELU_AFTER = 3

SUM_AFTER = 1

STEPS = ("1A", "1B", "2A", "0A", "2B", "0B")
Z = (PAIRS, 3)
PE = (len(PE_ORDER), 3)
HI = (len(SPLIT), 1)
LO_DVE = (len(SPLIT_DVE), 1)
LO_POOL = (len(SPLIT_POOL), 0)
RING = (PAIRS, 2)
Y = (1, 1)
Z0 = {"rest": 0, 0: 1, 1: 2}
PE0 = {0: 0, "rest": 1, 1: 2}
DVE_LOWS = [int(x[1:]) for x in DVE_ORDER if x[0] == "d"]
H_AT = {"1A": 0, "1B": 1, "0A": 2, "0B": 3}
Y_BANKS = 3


def total(counts):
    return 4 * counts[0] + 2 * counts[1]


def before(step, counts):
    return sum(counts[s[0] == "0"] for s in STEPS[:STEPS.index(step)])


def is_last(it):
    return isinstance(it, int) and it == ITERS - 1


def done(it, counts, step, k=0):
    missing = counts[1] if is_last(it) and step == "2B" else 0
    return (it + 1) * total(counts) + before(step, counts) - missing + k + 1


def h_done(it, step):
    return (it + 1) * 4 + H_AT[step] + 1


def back(it, step, k, counts, n):
    start = before(step, counts) + k - n
    prev = start < 0
    at = start + total(counts) * prev
    for s in STEPS:
        size = counts[s[0] == "0"]
        if at < size:
            if s == "0A" and is_last(it - prev):
                return back(it, step, k - n, counts, n)
            return it - prev, s, at
        at -= size


def build(nc, dense_t, ids_d, tables, w0_d, w0m_d, w16_d, w16m_d, w_split_d, w_native_d, bias_d,
          top_w1, top_b1, top_w2, top_b2, top_w3, out_d):
    with ExitStack() as ctx:
        def sb(name, shape, dt=F32):
            return ctx.enter_context(nc.sbuf_tensor(name, shape, dt))

        def ps(name, shape):
            return ctx.enter_context(nc.psum_tensor(name, shape, F32))

        def sem(name):
            return ctx.enter_context(nc.semaphore(name))

        NS, NN = len(SPLIT), len(NATIVE)
        ids_all = sb("ids_all", [P, BLOCKS, FIELDS], I32)
        ids_now = sb("ids_now", [P, FIELDS], I32)
        gathered = sb("gathered", [P, FIELDS, EMB])
        ident = sb("ident", [P, P])
        x4 = sb("x4", [P, 2 * CHUNK])
        z_ring = sb("z_ring", [P, Z_RING, 2 * CHUNK])
        zhi = sb("zhi", [P, S_RING, 2 * CHUNK], F32R)
        zlo = sb("zlo", [P, S_RING, 2 * CHUNK], F32R)
        z16 = sb("z16", [96, CHUNK])
        z16s = sb("z16s", [96, CHUNK], F32R)
        w0 = sb("w0", [P, 4, P])
        w16 = sb("w16", [96, P])
        w16s = sb("w16s", [96, P], F32R)
        w_nat = sb("w_nat", [P, 2, 2 * NN, P])
        w_hi = sb("w_hi", [P, 2, 2 * NS, P], F32R)
        w_lo = sb("w_lo", [P, 2, 2 * NS, P], F32R)
        bias = sb("bias", [P, 3])
        kept = [sb(f"kept_{c}", [P, 2, CHUNK]) for c in "ab"]
        block_sum = sb("block_sum", [P, 2, P])
        zsum = sb("zsum", [P, 2, BATCH])
        xrep_a = sb("xrep_a", [P, FIELDS // 2, CHUNK])
        iterations = ExitStack()

        def sb_iterations(name, shape):
            return iterations.enter_context(nc.sbuf_tensor(name, shape, F32))

        g4 = sb_iterations("g4", [P, EMB, P])
        rot = sb_iterations("rot", [P, 4, 2 * CHUNK])
        rot16 = sb_iterations("rot16", [96, 2 * CHUNK])
        xrep = [xrep_a, sb_iterations("xrep_b", [P, FIELDS // 2, CHUNK])]
        stage = 4 * NS * P
        top_b = xrep[1][:, :, :].rearrange("p t n -> p (t n)")
        w_stage = top_b[:, 0:stage].rearrange("p (l t o) -> p l t o", l=2, t=2 * NS)
        w0m = top_b[:, stage:stage + 4 * P].rearrange("p (j o) -> p j o", j=4)
        w16m = top_b[0:96, stage + 4 * P:stage + 5 * P]
        iterations.close()
        n1, n2 = 2 * TOP1, 4 * TOP2
        assert EMB * P == 2 * BATCH and 4 * 2 * CHUNK == 2 * (n1 + n2) and 2 * CHUNK == BATCH
        sum_hi = sb("sum_hi", [P, 2, BATCH], F32R)
        t1_hi = sb("t1_hi", [P, 2, TOP1], F32R)
        t1_lo = sb("t1_lo", [P, 2, TOP1], F32R)
        t2_hi = sb("t2_hi", [P, 4, TOP2], F32R)
        t2_lo = sb("t2_lo", [P, 4, TOP2], F32R)
        dense_s = sb("dense_s", [3 * DENSE, BATCH], F32R)
        sum_lo = sb("sum_lo", [P, 2, BATCH], F32R)
        a1 = sb("a1", [P, 4, BATCH])
        a2 = sb("a2", [P, 2, BATCH])
        td_s = z16s[0:3 * DENSE, :]
        a1_hi, a1_lo = zhi, zlo
        y_out = x4[0:1, :]
        top_a = xrep_a[:, :, :].rearrange("p t n -> p (t n)")
        t1 = top_a[:, 0:n1].rearrange("p (k n) -> p k n", k=2)
        t2 = top_a[:, n1:n1 + n2].rearrange("p (k n) -> p k n", k=4)
        base = n1 + n2
        t3 = top_a[:, base:base + 2]
        tb1 = top_a[:, base + 2:base + 6]
        tb2 = top_a[:, base + 6:base + 8]
        base += 8
        dense = top_a[0:3 * DENSE, base:base + BATCH]
        td = top_a[0:3 * DENSE, base + BATCH:base + BATCH + TOP1]
        x_dram = [nc.dram_tensor(f"x_dram_{h}", [2 * FIELDS, 2 * CHUNK], F32, kind="Internal").ap()
                  for h in range(2)]

        y = [ps(f"y_{n}", [P, CHUNK]) for n in range(Y_BANKS)]
        h = [ps(f"h_{c}", [P, CHUNK]) for c in "ab"]
        xt = ps("xt", [P, 2 * CHUNK])

        def y_of(step):
            return y[STEPS.index(step) % Y_BANKS]

        def top_bank(n):
            return [xt[:, 0:CHUNK], xt[:, CHUNK:], h[0][:, :], h[1][:, :],
                    y[0][:, :], y[2][:, :], y[1][:, :]][n]

        ids_in = sem("ids_in")
        weights_in = sem("weights_in")
        native_in = sem("native_in")
        memset_done = sem("memset_done")
        ident_ready = sem("ident_ready")
        whi_ready = sem("whi_ready")
        wlo_ready = sem("wlo_ready")
        w0_ready = sem("w0_ready")
        ids_copied = sem("ids_copied")
        rows_gathered = sem("rows_gathered")
        g4_ready = sem("g4_ready")
        xt_ready = sem("xt_ready")
        x4_ready = sem("x4_ready")
        x_stored = sem("x_stored")
        rot16_first = sem("rot16_first")
        rot_first = [[sem(f"rot_first_{c}{n}") for n in range(2)] for c in "ab"]
        rot_in = sem("rot_in")
        xrep_in = [[sem(f"xrep_in_{c}{q}") for q in range(4)] for c in "ab"]
        z_ready = sem("z_ready")
        hi_ready = sem("hi_ready")
        lo_dve_ready = sem("lo_dve_ready")
        lo_pool_ready = sem("lo_pool_ready")
        pe_done = sem("pe_done")
        h_ready = sem("h_ready")
        y_read = sem("y_read")
        folded = sem("folded")
        sum_ready = sem("sum_ready")
        top_in = sem("top_in")
        top_hi = sem("top_hi")
        top_lo = sem("top_lo")
        top_mm = sem("top_mm")
        a1_low = sem("a1_low")
        top_act = sem("top_act")
        out_stored = sem("out_stored")

        TOP_LOADS = 1 + 6 + 4
        T1, TD, DENSE_S, SUM, T2, SUM_LAST = range(1, 7)
        assert 4 * BATCH == S_RING * 2 * CHUNK
        ROTS = 3 + 4
        def slot(step, k):
            return (before(step, (NS, 0)) + k) % S_RING

        def z_pair_of(step, i):
            return z_ring[:, (before(step, RING) + i) % Z_RING, :]

        def low_slot_free(eng, it, step, k):
            at, s, n = back(it, step, k, (NS, 0), S_RING)
            eng.wait_ge(pe_done, done(at, PE, s, PE_ORDER.index(f"L{SPLIT[n]}")))

        def low_made(eng, it, step, i):
            if i in SPLIT_POOL:
                eng.wait_ge(lo_pool_ready, done(it, LO_POOL, step, SPLIT_POOL.index(i)))
            else:
                eng.wait_ge(lo_dve_ready, done(it, LO_DVE, step, DVE_LOWS.index(i)))

        block = ctx.enter_context(nc.Block())

        @block.sync
        def _(sp):
            sp.dma_start(ids_all[:, :, :], ids_d).then_inc(ids_in, 16)
            sp.dma_start(w_stage, w_split_d).then_inc(weights_in, 16)
            sp.dma_start(w0[:, :, :], w0_d).then_inc(weights_in, 16)
            sp.dma_start(w0m, w0m_d).then_inc(weights_in, 16)
            sp.dma_start(w16[:, :], w16_d).then_inc(weights_in, 16)
            sp.dma_start(w16m, w16m_d).then_inc(weights_in, 16)
            sp.dma_start(w_nat[:, :, :, :], w_native_d).then_inc(native_in, 16)
            sp.dma_start(bias[:, :], bias_d).then_inc(native_in, 16)

            def x_rows(half, row, steps, cols):
                return bass.AP(tensor=x_dram[half].tensor, offset=row * 2 * CHUNK + cols.start,
                               ap=[[step * 2 * CHUNK, n] for step, n in steps] +
                                  [[1, cols.stop - cols.start]])

            def rotate16(signal):
                for r in range(3):
                    sp.dma_start(rot16[FIELDS * r:FIELDS * (r + 1), :],
                                 x4[16:16 + FIELDS, :]).then_inc(signal, 16)

            def rotate(half, cols, signals):
                for j in range(4):
                    sp.dma_start(rot[:, j, cols], x_rows(half, 4 * j, [(1, 4), (1, FIELDS)],
                                                         cols)).then_inc(signals[j // 2], 16)

            def replicate(it, half, c, first=False):
                for q in range(4):
                    if first and c == 1 and q == 0:
                        sp.wait_ge(wlo_ready, 1)
                        sp.wait_ge(whi_ready, 1)
                        sp.wait_ge(w0_ready, 2)
                    if not first:
                        sp.wait_ge(z_ready, done(it - 1, Z, "2" + "AB"[c], 2 * q + 1))
                    for j in range(2):
                        sp.dma_start(xrep[c][HALF * j:HALF * (j + 1), 4 * q:4 * q + 4, :],
                                     x_rows(half, 8 * q + j, [(0, HALF), (2, 4)],
                                            slice(c * CHUNK, (c + 1) * CHUNK))
                                     ).then_inc(xrep_in[c][q], 16)

            def store_x(it, half, signal):
                sp.wait_ge(x4_ready, it + 1)
                sp.dma_start(x_dram[half], x4[0:2 * FIELDS, :]).then_inc(x_stored, 16)
                rotate16(signal)
                sp.wait_ge(x_stored, 16 * (it + 1))

            def fetch_x(it, half):
                store_x(it, half, rot_in)
                rotate(half, slice(0, 2 * CHUNK), [rot_in] * 2)
                for c in range(2):
                    replicate(it, half, c)

            store_x(0, 0, rot16_first)
            for c in range(2):
                rotate(0, slice(c * CHUNK, (c + 1) * CHUNK), rot_first[c])
            for c in range(2):
                replicate(0, 0, c, first=True)
            with sp.Fori(0, BLOCKS - 1) as m:
                fetch_x(2 * m + 1, 1)
                fetch_x(2 * m + 2, 0)
            fetch_x(ITERS - 1, 1)
            sp.wait_ge(z_ready, done(ITERS - 1, Z, "2A", PAIRS - 1))
            sp.dma_start(t1, top_w1[0:2 * P, :].rearrange("(k p) n -> p k n", p=P)
                         ).then_inc(top_in, 16)
            for r in range(3):
                rows = slice(r * DENSE, (r + 1) * DENSE)
                sp.dma_start(td[rows, :], top_w1[2 * P:2 * P + DENSE, :]).then_inc(top_in, 16)
                sp.dma_start(dense[rows, :], dense_t).then_inc(top_in, 16)
            sp.dma_start(t2, top_w2.rearrange("(k p) n -> p k n", p=P)).then_inc(top_in, 16)
            sp.dma_start(t3, top_w3).then_inc(top_in, 16)
            sp.dma_start(tb1, top_b1).then_inc(top_in, 16)
            sp.dma_start(tb2, top_b2).then_inc(top_in, 16)
            sp.wait_ge(top_act, 8 + 4 + 2)
            sp.dma_start(out_d.rearrange("n a -> a n"), y_out).then_inc(out_stored, 16)
            sp.wait_ge(out_stored, 16)

        @block.gpsimd
        def _(pool):
            def gather(f0, f1):
                for f in range(f0, f1):
                    nc.gpsimd.indirect_dma_start(
                        out=gathered[:, f, :], out_offset=None, in_=tables[f],
                        in_offset=bass.IndirectOffsetOnAxis(ap=ids_now[:, f:f + 1], axis=0),
                    ).then_inc(rows_gathered, 16)

            def next_ids(blk):
                pool.wait_ge(g4_ready, 2 * blk)
                nc.gpsimd.tensor_copy(ids_now[:, :], ids_all[:, blk, :]).then_inc(ids_copied, 1)
                pool.wait_ge(ids_copied, blk + 1)

            pool.sem_inc(lo_pool_ready, total(LO_POOL))
            pool.sem_inc(sum_ready, 2)
            pool.wait_ge(ids_in, 16)
            nc.gpsimd.tensor_copy(ids_now[:, :], ids_all[:, 0, :]).then_inc(ids_copied, 1)
            pool.wait_ge(ids_copied, 1)
            gather(0, 8)
            nc.gpsimd.memset(ident[:, :], 0.0).then_inc(memset_done, 1)
            pool.wait_ge(memset_done, 1)
            nc.gpsimd.affine_select(out=ident[:, :], in_=ident[:, :], compare_op=ALU.not_equal,
                                    fill=1.0, base=0, pattern=[[-1, P]],
                                    channel_multiplier=1).then_inc(ident_ready, 1)
            gather(8, FIELDS)
            next_ids(1)
            gather(0, 12)

            def low(it, step, i):
                k = SPLIT.index(i)
                s = slot(step, k)
                pool.wait_ge(hi_ready, done(it, HI, step, k))
                low_slot_free(pool, it, step, k)
                nc.gpsimd.tensor_tensor(zlo[:, s, :], z_pair_of(step, i), zhi[:, s, :].bitcast(F32),
                                        ALU.subtract).then_inc(lo_pool_ready, 1)

            def sum_chunk(it, par, blk, c, folds):
                pool.wait_ge(y_read, done(it, Y, "2" + "AB"[c]))
                v = kept[c]
                nc.gpsimd.tensor_tensor(v[:, :, 0:2 * P], v[:, :, 0:2 * P], v[:, :, 2 * P:4 * P],
                                        ALU.add).then_inc(folded, 1)
                pool.wait_ge(folded, folds + 1)
                if par == 0 and c == 0:
                    pool.wait_ge(sum_ready, 2 * it + 2)
                    nc.gpsimd.tensor_tensor(block_sum[:, :, :], v[:, :, 0:P], v[:, :, P:2 * P],
                                            ALU.add).then_inc(sum_ready, 1)
                    return
                nc.gpsimd.tensor_tensor(v[:, :, 0:P], v[:, :, 0:P], v[:, :, P:2 * P],
                                        ALU.add).then_inc(folded, 1)
                pool.wait_ge(folded, folds + 2)
                pool.wait_ge(sum_ready, 2 * it + 2 + c)
                out = zsum[:, :, bass.ts(blk, P)] if par == 1 and c == 1 else block_sum[:, :, :]
                nc.gpsimd.tensor_tensor(out, block_sum[:, :, :], v[:, :, 0:P],
                                        ALU.add).then_inc(sum_ready, 1)

            ODD = {"1B": (0, 4), "2A": (4, 8), "2B": (8, 12)}
            EVEN = {"1A": (12, 17), "1B": (17, 22), "2A": (22, 27), "2B": (27, FIELDS)}

            def body(it, par, blk, gathers):
                for step in STEPS:
                    if step[0] != "0":
                        for k, i in enumerate(SPLIT_POOL):
                            if k == 2 and step == "1B" and par == 1 and gathers:
                                next_ids(blk + 2)
                            low(it, step, i)
                            if step == "2B" and k == 0:
                                sum_chunk(it, par, blk, 0, 7 * blk + 3 * par)
                    if gathers and step in gathers:
                        gather(*gathers[step])
                sum_chunk(it, par, blk, 1, 7 * blk + 3 * par + 1 + par)

            with pool.Fori(0, BLOCKS - 2) as m:
                body(2 * m, 0, m, EVEN)
                body(2 * m + 1, 1, m, ODD)
            body(ITERS - 4, 0, BLOCKS - 2, EVEN)
            body(ITERS - 3, 1, BLOCKS - 2, None)
            body(ITERS - 2, 0, BLOCKS - 1, None)
            body(ITERS - 1, 1, BLOCKS - 1, None)

        @block.scalar
        def _(act):
            def high(it, step, i):
                k = SPLIT.index(i)
                act.wait_ge(z_ready, done(it, Z, step, i))
                at, s, n = back(it, step, k, (NS, 0), S_RING)
                act.wait_ge(pe_done, done(at, PE, s, PE_ORDER.index(f"H{SPLIT[n]}")))
                low_made(act, at, s, SPLIT[n])
                nc.scalar.activation(zhi[:, slot(step, k), :], z_pair_of(step, i),
                                     ACT.Copy).then_inc(hi_ready, 1)

            def high16(it, step, first=False):
                act.wait_ge(z_ready, done(it, Z, step, Z0["rest"]))
                if step == "0B":
                    act.wait_ge(pe_done, done(it, PE, "0A", PE0["rest"]))
                elif not first:
                    act.wait_ge(pe_done, done(it - 1, PE, "0B", PE0["rest"]))
                nc.scalar.activation(z16s[:, :], z16[:, :], ACT.Copy).then_inc(hi_ready, 1)

            up, down = slice(HALF, P), slice(0, HALF)

            def relu(it, step):
                layer, c = int(step[0]), "AB".index(step[1])
                act.wait_ge(pe_done, done(it, PE, step, PE[layer == 0] - 1))
                yy = y_of(step)
                if layer == 2:
                    nc.scalar.activation(kept[c][:, 1, :], yy[:, :], ACT.Relu,
                                         bias=bias[:, 2:3]).then_inc(y_read, 1)
                    return
                on, off = (up, down) if layer == 0 else (down, up)
                nc.scalar.activation(h[c][on, :], yy[on, :], ACT.Relu, bias=bias[on, layer:layer + 1])
                nc.scalar.activation(h[c][off, :], yy[on, :], ACT.Relu,
                                     bias=bias[on, layer:layer + 1]).then_inc(h_ready, 1)
                if layer == 0:
                    act.wait_ge(sum_ready, 2 * (it + 1) + c + 1)
                nc.scalar.activation(kept[c][off, 0, :], yy[off, :], ACT.Relu,
                                     bias=bias[off, layer:layer + 1]).then_inc(y_read, 1)

            def spread(blk):
                act.wait_ge(rows_gathered, 16 * FIELDS * (blk + 1))
                for e0 in range(0, EMB, 8):
                    nc.scalar.activation(
                        g4[:, e0:e0 + 8, :].rearrange("p e (r f) -> p e r f", r=4),
                        gathered[:, :, e0:e0 + 8].rearrange("p f e -> p e f")[:, :, None, :]
                        .to_broadcast([P, 8, 4, FIELDS]), ACT.Copy).then_inc(g4_ready, 1)

            def evacuate(it):
                act.wait_ge(xt_ready, it + 1)
                nc.scalar.activation(x4[:, :], xt[:, :], ACT.Copy).then_inc(x4_ready, 1)

            def top_high():
                act.wait_ge(top_in, 16 * TOP_LOADS)
                act.wait_ge(sum_ready, 2 + ITERS)
                for hi, whole in ((t1_hi[:, :, :], t1), (td_s, td), (dense_s[:, :], dense),
                                  (sum_hi[:, :, 0:CHUNK], zsum[:, :, 0:CHUNK]),
                                  (t2_hi[:, :, :], t2)):
                    nc.scalar.activation(hi, whole, ACT.Copy).then_inc(top_hi, 1)

            act.sem_inc(hi_ready, before("0A", HI))
            act.sem_inc(h_ready, 2)
            act.sem_inc(y_read, 3)
            act.wait_ge(weights_in, 5 * 16)
            nc.scalar.activation(w_hi[:, :, :, :], w_stage, ACT.Copy).then_inc(whi_ready, 1)
            act.wait_ge(w0_ready, 2)
            nc.scalar.activation(w16s[:, :], w16[:, :], ACT.Copy).then_inc(whi_ready, 1)
            act.wait_ge(native_in, 32)
            spread(0)
            evacuate(0)
            high16(-1, "0A", first=True)
            act.wait_ge(hi_ready, done(-1, HI, "0A"))
            act.sem_inc(hi_ready, HI[0])
            high16(-1, "0B")
            relu(-1, "0A")
            act.wait_ge(y_read, done(-1, Y, "0A"))
            act.sem_inc(y_read, 1)

            def body(it, par, m, last):
                for step, earlier in zip(STEPS, (None,) + STEPS):
                    if step[0] == "0":
                        if not last:
                            high16(it, step)
                            if step == "0A":
                                relu(it, "2A")
                        elif step == "0A":
                            relu(it, "2A")
                        if step == "0B":
                            if last:
                                top_high()
                            relu(it, "2B")
                        continue
                    for k, i in enumerate(SPLIT):
                        if k == RELU_AFTER:
                            if step == "1A":
                                relu(it - 1, "0B")
                            elif step != "2B" or not last:
                                relu(it, earlier)
                            if step == "1B" and not last:
                                evacuate(it + 1)
                        high(it, step, i)
                    if step == "1A" and par == 1 and not last:
                        act.wait_ge(xt_ready, 2 * m + 2)
                        spread(m + 1)

            with act.Fori(0, BLOCKS - 1) as m:
                body(2 * m, 0, m, False)
                body(2 * m + 1, 1, m, False)
            body(ITERS - 2, 0, BLOCKS - 1, False)
            body(ITERS - 1, 1, BLOCKS - 1, True)
            for n in range(2):
                cols = slice(n * CHUNK, (n + 1) * CHUNK)
                for m in range(4):
                    act.wait_ge(top_mm, 4 * n + m + 1)
                    bank = top_bank((4 * n + m) % 7)
                    nc.scalar.activation(a1[:, m, cols], bank, ACT.Relu, bias=tb1[:, m:m + 1])
                    nc.scalar.activation(a1_hi[:, m, cols], bank, ACT.Relu,
                                         bias=tb1[:, m:m + 1]).then_inc(top_act, 1)
                    if n == 0 and m == SUM_AFTER:
                        act.wait_ge(sum_ready, 2 + 2 * ITERS)
                        nc.scalar.activation(sum_hi[:, :, CHUNK:], zsum[:, :, CHUNK:],
                                             ACT.Copy).then_inc(top_hi, 1)
            for n in range(2):
                for m in range(2):
                    act.wait_ge(top_mm, 8 + 2 * n + m + 1)
                    nc.scalar.activation(a2[:, m, n * CHUNK:(n + 1) * CHUNK],
                                         top_bank(1 + 2 * n + m), ACT.Relu,
                                         bias=tb2[:, m:m + 1]).then_inc(top_act, 1)
            for n in range(2):
                act.wait_ge(top_mm, 12 + n + 1)
                nc.scalar.activation(y_out[:, n * CHUNK:(n + 1) * CHUNK],
                                     top_bank(5 + n)[0:1, :], ACT.Copy).then_inc(top_act, 1)

        @block.vector
        def _(dve):
            dve.sem_inc(z_ready, before("0A", Z))
            dve.sem_inc(lo_dve_ready, before("0A", LO_DVE))
            dve.wait_ge(weights_in, 5 * 16)
            nc.vector.tensor_tensor(w0[:, :, :], w0[:, :, :], w0m, ALU.add).then_inc(w0_ready, 1)
            nc.vector.tensor_tensor(w16[:, :], w16[:, :], w16m, ALU.add).then_inc(w0_ready, 1)
            dve.wait_ge(whi_ready, 1)
            nc.vector.tensor_tensor(w_lo[:, :, :, :], w_stage, w_hi[:, :, :, :].bitcast(F32),
                                    ALU.subtract).then_inc(wlo_ready, 1)
            dve.wait_ge(whi_ready, 2)
            nc.vector.tensor_tensor(w16s[HALF:96, :], w16[HALF:96, :],
                                    w16s[HALF:96, :].bitcast(F32),
                                    ALU.subtract).then_inc(wlo_ready, 1)

            def slot_free(it, step, i):
                at, s, n = back(it, step, i, RING, Z_RING)
                if s[0] == "0":
                    dve.wait_ge(pe_done, done(at, PE, s, PE0[n]))
                elif n in NATIVE:
                    dve.wait_ge(pe_done, done(at, PE, s, PE_ORDER.index(f"N{n}")))
                else:
                    low_made(dve, at, s, n)

            def z_pair(it, step, i):
                c = "AB".index(step[1])
                if i == 0:
                    dve.wait_ge(h_ready, h_done(it - 1, "0" + step[1]) if step[0] == "1" else
                                h_done(it, "1" + step[1]))
                if step[0] == "1" and i % 2 == 0:
                    dve.wait_ge(xrep_in[c][i // 2], 32 * (it + 1))
                slot_free(it, step, i)
                nc.vector.tensor_tensor(
                    z_pair_of(step, i).rearrange("p (t n) -> p t n", t=2),
                    xrep[c][:, 2 * i:2 * i + 2, :],
                    h[c][:, None, :].to_broadcast([P, 2, CHUNK]), ALU.mult).then_inc(z_ready, 1)

            def low(it, step, i):
                k = SPLIT.index(i)
                s = slot(step, k)
                dve.wait_ge(hi_ready, done(it, HI, step, k))
                low_slot_free(dve, it, step, k)
                nc.vector.tensor_tensor(zlo[:, s, :], z_pair_of(step, i), zhi[:, s, :].bitcast(F32),
                                        ALU.subtract).then_inc(lo_dve_ready, 1)

            def layer0(it, step, first=False):
                c = "AB".index(step[1])
                cols = slice(c * CHUNK, (c + 1) * CHUNK)
                if first:
                    dve.wait_ge(rot16_first, 3 * 16)
                elif step == "0A":
                    dve.wait_ge(rot_in, 16 * ROTS * (it + 1))
                other = (it - 1, "0B") if step == "0A" else (it, "0A")
                dve.wait_ge(lo_dve_ready, done(other[0], LO_DVE, other[1]))
                nc.vector.tensor_tensor(z16[:, :], rot16[:, cols], x4[0:96, cols],
                                        ALU.mult).then_inc(z_ready, 1)
                for i in range(2):
                    if first:
                        dve.wait_ge(rot_first[c][i], 2 * 16)
                    else:
                        slot_free(it, step, i)
                    nc.vector.tensor_tensor(
                        z_pair_of(step, i).rearrange("p (t n) -> p t n", t=2),
                        rot[:, 2 * i:2 * i + 2, cols],
                        x4[:, None, cols].to_broadcast([P, 2, CHUNK]),
                        ALU.mult).then_inc(z_ready, 1)
                    if i == 0:
                        dve.wait_ge(hi_ready, done(it, HI, step))
                        mid = slice(FIELDS, HALF)
                        nc.vector.tensor_tensor(z16s[mid, :], z16[mid, :], z16s[mid, :].bitcast(F32),
                                                ALU.subtract).then_inc(lo_dve_ready, 1)

            dve.wait_ge(x4_ready, 1)
            layer0(-1, "0A", first=True)
            dve.wait_ge(z_ready, done(-1, Z, "0A", 2))
            dve.wait_ge(lo_dve_ready, done(-1, LO_DVE, "0A"))
            dve.sem_inc(z_ready, Z[0])
            dve.sem_inc(lo_dve_ready, LO_DVE[0])
            layer0(-1, "0B", first=True)

            def body(it, last):
                for step in STEPS:
                    if step[0] == "0":
                        if not last:
                            layer0(it, step)
                        continue
                    for item in DVE_ORDER:
                        (z_pair if item[0] == "z" else low)(it, step, int(item[1:]))

            with dve.Fori(0, BLOCKS - 1) as m:
                body(2 * m, False)
                body(2 * m + 1, False)
            body(ITERS - 2, False)
            body(ITERS - 1, True)

            def top_low(n, low, whole, hi):
                dve.wait_ge(top_hi, n)
                nc.vector.tensor_tensor(low, whole, hi.bitcast(F32), ALU.subtract
                                        ).then_inc(top_lo, 1)

            top_low(T1, t1_lo[:, :, :], t1, t1_hi[:, :, :])
            top_low(TD, td_s[0:DENSE, :], td[0:DENSE, :], td_s[0:DENSE, :])
            third = slice(2 * DENSE, 3 * DENSE)
            top_low(DENSE_S, dense_s[third, :], dense[third, :], dense_s[third, :])
            dve.wait_ge(z_ready, done(ITERS - 1, Z, "2B", PAIRS - 1))
            top_low(SUM, sum_lo[:, :, 0:CHUNK], zsum[:, :, 0:CHUNK], sum_hi[:, :, 0:CHUNK])
            top_low(T2, t2_lo[:, :, :], t2, t2_hi[:, :, :])
            for n in range(2):
                cols = slice(n * CHUNK, (n + 1) * CHUNK)
                for m in range(4):
                    dve.wait_ge(top_act, 4 * n + m + 1)
                    nc.vector.tensor_tensor(a1_lo[:, m, cols], a1[:, m, cols],
                                            a1_hi[:, m, cols].bitcast(F32), ALU.subtract
                                            ).then_inc(a1_low, 1)
                    if n == 0 and m == SUM_AFTER:
                        top_low(SUM_LAST, sum_lo[:, :, CHUNK:], zsum[:, :, CHUNK:],
                                sum_hi[:, :, CHUNK:])

        @block.tensor
        def _(pe):
            def transpose_x(it, half):
                for k in range(2 * CHUNK_E):
                    op = nc.tensor.matmul(xt[:, k * P:(k + 1) * P],
                                          g4[:, 2 * CHUNK_E * half + k, :], ident[:, :],
                                          start=True, stop=True, is_transpose=True)
                op.then_inc(xt_ready, 1)

            def y_free(it, step):
                at, s, _ = back(it, step, 0, Y, Y_BANKS)
                pe.wait_ge(y_read, done(at, Y, s))

            def layer0(it, step):
                y_free(it, step)
                yy = y_of(step)
                for i in range(2):
                    pe.wait_ge(z_ready, done(it, Z, step, Z0[i]))
                    for k in range(2):
                        op = nc.tensor.matmul(yy[:, :], w0[:, 2 * i + k, :],
                                              z_pair_of(step, i)[:, k * CHUNK:(k + 1) * CHUNK],
                                              start=(i == 0 and k == 0), stop=(i == 1 and k == 1))
                    op.then_inc(pe_done, 1)
                    if i == 0:
                        pe.wait_ge(lo_dve_ready, done(it, LO_DVE, step))
                        nc.tensor.matmul(yy[:, :], w16s[:, :], z16s[:, :], start=False,
                                         stop=False).then_inc(pe_done, 1)

            def item_of(it, step, item):
                kind, i = item[0], int(item[1:])
                layer = int(step[0]) - 1
                first, final = item == PE_ORDER[0], item == PE_ORDER[-1]
                if kind == "N":
                    pe.wait_ge(z_ready, done(it, Z, step, i))
                    n = NATIVE.index(i)
                    terms = [(w_nat[:, layer, 2 * n + k, :], z_pair_of(step, i), k)
                             for k in range(2)]
                else:
                    n = SPLIT.index(i)
                    s = slot(step, n)
                    if kind == "H":
                        pe.wait_ge(hi_ready, done(it, HI, step, n))
                        terms = [(w[:, layer, 2 * n + k, :], zhi[:, s, :], k)
                                 for k in range(2) for w in (w_hi, w_lo)]
                    else:
                        low_made(pe, it, step, i)
                        terms = [(w_hi[:, layer, 2 * n + k, :], zlo[:, s, :], k) for k in range(2)]
                for t, (w, z, k) in enumerate(terms):
                    op = nc.tensor.matmul(y_of(step)[:, :], w, z[:, k * CHUNK:(k + 1) * CHUNK],
                                          start=(first and t == 0),
                                          stop=(final and t == len(terms) - 1))
                op.then_inc(pe_done, 1)

            pe.sem_inc(pe_done, before("0A", PE))
            pe.wait_ge(ident_ready, 1)
            pe.wait_ge(g4_ready, 1)
            transpose_x(0, 0)
            pe.wait_ge(w0_ready, 2)
            pe.wait_ge(wlo_ready, 2)
            layer0(-1, "0A")
            pe.wait_ge(pe_done, done(-1, PE, "0A", 2))
            pe.sem_inc(pe_done, PE[0])
            layer0(-1, "0B")
            pe.wait_ge(native_in, 32)

            def body(it, par, m, last):
                for step in STEPS:
                    if step[0] == "0":
                        if not last:
                            layer0(it, step)
                        continue
                    y_free(it, step)
                    for item in PE_ORDER:
                        item_of(it, step, item)
                    if step == "1A" and not last:
                        pe.wait_ge(g4_ready, 2 * (m + par) + 2 - par)
                        transpose_x(it + 1, 1 - par)

            with pe.Fori(0, BLOCKS - 1) as m:
                body(2 * m, 0, m, False)
                body(2 * m + 1, 1, m, False)
            body(ITERS - 2, 0, BLOCKS - 1, False)
            body(ITERS - 1, 1, BLOCKS - 1, True)

            for n in range(2):
                cols = slice(n * CHUNK, (n + 1) * CHUNK)
                pe.wait_ge(top_hi, SUM_LAST if n else SUM)
                for m in range(4):
                    out = slice(m * P, (m + 1) * P)
                    if 4 * n + m == 6:
                        pe.wait_ge(y_read, done(ITERS - 1, Y, "2B") - 1)
                    if 4 * n + m == 7:
                        pe.wait_ge(top_act, 1)
                    bank = top_bank((4 * n + m) % 7)
                    for k in range(2):
                        if m == 0 and k == 0:
                            pe.wait_ge(top_lo, DENSE_S)
                        nc.tensor.matmul(bank, t1_lo[:, k, out], sum_hi[:, k, cols],
                                         start=(k == 0), stop=False)
                        nc.tensor.matmul(bank, t1_hi[:, k, out], sum_hi[:, k, cols],
                                         start=False, stop=False)
                    nc.tensor.matmul(bank, td_s[:, out], dense_s[:, cols], start=False, stop=False)
                    if m == 0:
                        pe.wait_ge(top_lo, SUM_LAST if n else SUM)
                    for k in range(2):
                        op = nc.tensor.matmul(bank, t1_hi[:, k, out], sum_lo[:, k, cols],
                                              start=False, stop=(k == 1))
                    op.then_inc(top_mm, 1)
            for n in range(2):
                cols = slice(n * CHUNK, (n + 1) * CHUNK)
                if n == 0:
                    pe.wait_ge(top_lo, T2)
                for m in range(2):
                    out = slice(m * P, (m + 1) * P)
                    bank = top_bank(1 + 2 * n + m)
                    for k in range(4):
                        if m == 0:
                            pe.wait_ge(top_act, 4 * n + k + 1)
                        nc.tensor.matmul(bank, t2_lo[:, k, out], a1_hi[:, k, cols],
                                         start=(k == 0), stop=False)
                        nc.tensor.matmul(bank, t2_hi[:, k, out], a1_hi[:, k, cols],
                                         start=False, stop=False)
                    for k in range(4):
                        if m == 0:
                            pe.wait_ge(a1_low, 4 * n + k + 1)
                        op = nc.tensor.matmul(bank, t2_hi[:, k, out], a1_lo[:, k, cols],
                                              start=False, stop=(k == 3))
                    op.then_inc(top_mm, 1)
            pe.wait_ge(top_in, 16 * TOP_LOADS)
            for n in range(2):
                cols = slice(n * CHUNK, (n + 1) * CHUNK)
                pe.wait_ge(top_act, 8 + 2 * n + 2)
                for k in range(2):
                    op = nc.tensor.matmul(top_bank(5 + n)[0:1, :], t3[:, k:k + 1], a2[:, k, cols],
                                          start=(k == 0), stop=(k == 1))
                op.then_inc(top_mm, 1)


def kernel(**inputs):
    import numpy as np
    import concourse.bacc as bacc
    from concourse.bass_utils import run_bass_kernel_spmd

    a = {k: np.asarray(v) for k, v in inputs.items()}
    swap = np.r_[HALF:P, 0:HALF]
    g = np.arange(FIELDS)
    d = np.arange(16)
    w0 = a["L0_rec_W0"].reshape(P, FIELDS, FIELDS)
    near = (g[None, :] + d[:, None]) % FIELDS
    rows = np.broadcast_to(g[None, :], near.shape)
    tiles = lambda w: np.ascontiguousarray(
        w.reshape(P, 4, 4, FIELDS).transpose(2, 3, 1, 0).reshape(P, 4, P))
    mirror = w0[:, near, rows].copy()
    mirror[:, 0, :] = 0
    triple = np.zeros((2, 3, FIELDS, P), w0.dtype)
    low = np.arange(16)
    triple[0, :, :16, :] = w0[:, low, low + 16].T
    triple[1, :, :16, :] = w0[:, low + 16, low].T
    w12 = np.stack([a["L0_rec_W1"][swap], a["L0_rec_W2"]])
    w12 = w12.reshape(2, P, FIELDS // 2, P).transpose(3, 0, 2, 1)
    pick = lambda pairs: np.ascontiguousarray(w12[:, :, [2 * i + k for i in pairs for k in (0, 1)]])
    columns = lambda v: np.ascontiguousarray(v.reshape(-1, P).T)
    arrays = {
        "dense_t": np.ascontiguousarray(a["dense_ctx"].T),
        "ids": np.ascontiguousarray(a["ids"].reshape(BLOCKS, P, FIELDS).transpose(1, 0, 2)),
        "w0": tiles(w0[:, rows, near]), "w0m": tiles(mirror),
        "w16": triple[0].reshape(96, P), "w16m": triple[1].reshape(96, P),
        "w_split": pick(SPLIT), "w_native": pick(NATIVE),
        "bias": np.ascontiguousarray(np.stack([a["L0_rec_b0"], a["L0_rec_b1"][swap],
                                               a["L0_rec_b2"]], axis=1)),
        "top_w1": a["W_top1"], "top_b1": columns(a["b_top1"]), "top_w2": a["W_top2"],
        "top_b2": columns(a["b_top2"]), "top_w3": columns(a["W_top3"]),
        **{f"tbl_{f}": a[f"tbl_{f}"] for f in range(FIELDS)},
    }
    nc = bacc.Bacc("TRN2", target_bir_lowering=False, num_devices=1)
    ap = {k: nc.dram_tensor(f"in_{k}", v.shape, mybir.dt.from_np(v.dtype), kind="ExternalInput").ap()
          for k, v in arrays.items()}
    out = nc.dram_tensor("out_y", (BATCH, 1), F32, kind="ExternalOutput").ap()
    build(nc, ap["dense_t"], ap["ids"], [ap[f"tbl_{f}"] for f in range(FIELDS)], ap["w0"],
          ap["w0m"], ap["w16"], ap["w16m"], ap["w_split"], ap["w_native"], ap["bias"],
          ap["top_w1"], ap["top_b1"], ap["top_w2"], ap["top_b2"], ap["top_w3"], out)
    got = run_bass_kernel_spmd(nc, [{f"in_{k}": v for k, v in arrays.items()}], core_ids=[0])
    return got.results[0]["out_y"]
```
